# Optimizing a Trainium2 kernel written in Bass

```python
import numpy as np
import jax
import jax.numpy as jnp

def _softmax(x, axis=-1):
    return jax.nn.softmax(x, axis=axis)

def _gelu(x):
    return jax.nn.gelu(x, approximate=True)

def _silu(x):
    return jax.nn.silu(x)

def _sigmoid(x):
    return jax.nn.sigmoid(x)

def _layernorm(x, axis=-1, eps=1e-05):
    m = jnp.mean(x, axis=axis, keepdims=True)
    v = jnp.var(x, axis=axis, keepdims=True)
    return (x - m) / jnp.sqrt(v + eps)

def _scatter_add(tgt, idx, src, axis=0):
    return tgt.at[idx].add(src)

def _segment_sum(src, seg, n):
    return jax.ops.segment_sum(src, seg, n)
kernel_name = 'mk_early_fusion_d1_tok_img1024_r4_d7e3c1'

def setup_inputs(seed: int=0):
    np.random.seed(seed)
    _w = jnp.asarray

    def _rec_inputs():
        import jax
        import jax.numpy as jnp
        _rk = jax.random.key(seed)
        x = -0.00016672 + 0.999947 * jax.random.normal(jax.random.fold_in(_rk, 1), (32, 3, 96, 96), jnp.float32)
        txt = 0.00180885 + 1.15405 * jax.random.normal(jax.random.fold_in(_rk, 2), (32, 77, 256), jnp.float32)
        return (x, txt)
    x, txt = _rec_inputs()

    def _L0_tok_setup():
        import jax, jax.numpy as jnp
        import numpy as np
        B, C, H, W = (64, 3, 96, 96)
        P = 16
        HP, WP = (H // P, W // P)
        N = HP * WP
        F = C * P * P
        D = 256
        key = jax.random.key(seed)
        k1, k2, k3, k4, k5 = jax.random.split(key, 5)
        data = jax.random.normal(k1, (B, C, H, W), dtype=jnp.float32)
        lim = 1.0 / np.sqrt(F)
        W_lin = jax.random.uniform(k2, (D, F), minval=-lim, maxval=lim, dtype=jnp.float32)
        b_lin = jax.random.uniform(k3, (D,), minval=-lim, maxval=lim, dtype=jnp.float32)
        class_token = jax.random.normal(k4, (1, 1, D), dtype=jnp.float32)
        position_embeddings = jax.random.normal(k5, (1, N + 1, D), dtype=jnp.float32)
        return {'data': data, 'W_lin': W_lin, 'b_lin': b_lin, 'class_token': class_token, 'position_embeddings': position_embeddings}
    _L0_tok_all = _L0_tok_setup()
    _L0_tok_in = {k: v for k, v in _L0_tok_all.items() if k in ('W_lin', 'b_lin', 'class_token', 'position_embeddings')}
    del _L0_tok_all

    def _L0_attn_setup():
        import jax, jax.numpy as jnp
        import numpy as np
        WIN = 64
        STRIDE = 128
        HEADS = 16
        key = jax.random.key(seed)
        ks = jax.random.split(key, 5)
        B, S, D = (4, 1024, 256)
        scale = 0.02
        return {'hidden_states': jax.random.normal(ks[0], (B, S, D), jnp.float32), 'Wq': jax.random.normal(ks[1], (D, D), jnp.float32) * scale, 'Wk': jax.random.normal(ks[2], (D, D), jnp.float32) * scale, 'Wv': jax.random.normal(ks[3], (D, D), jnp.float32) * scale, 'Wo': jax.random.normal(ks[4], (D, D), jnp.float32) * scale}
    _L0_attn_all = _L0_attn_setup()
    _L0_attn_in = {k: v for k, v in _L0_attn_all.items() if k in ('Wq', 'Wk', 'Wv', 'Wo')}
    del _L0_attn_all

    def _L0_ffn_setup():
        import jax, jax.numpy as jnp
        import numpy as np
        NUM_EXPERTS = 8
        TOP_K = 2
        N_EMBD = 256
        B, T = (4, 512)
        key = jax.random.key(seed)
        k_x, k_g, k_e = jax.random.split(key, 3)
        x = jax.random.normal(k_x, (B, T, N_EMBD), dtype=jnp.float32)
        scale = 1.0 / np.sqrt(N_EMBD)
        gate_w = jax.random.uniform(k_g, (NUM_EXPERTS, N_EMBD), dtype=jnp.float32, minval=-scale, maxval=scale)
        expert_w = jax.random.uniform(k_e, (NUM_EXPERTS, N_EMBD, N_EMBD), dtype=jnp.float32, minval=-scale, maxval=scale)
        return {'x': x, 'gate_w': gate_w, 'expert_w': expert_w}
    _L0_ffn_all = _L0_ffn_setup()
    _L0_ffn_in = {k: v for k, v in _L0_ffn_all.items() if k in ('gate_w', 'expert_w')}
    del _L0_ffn_all
    return {'x': x, 'txt': txt, 'L0_tok_W_lin': _L0_tok_in['W_lin'], 'L0_tok_b_lin': _L0_tok_in['b_lin'], 'L0_tok_class_token': _L0_tok_in['class_token'], 'L0_tok_position_embeddings': _L0_tok_in['position_embeddings'], 'L0_attn_Wq': _L0_attn_in['Wq'], 'L0_attn_Wk': _L0_attn_in['Wk'], 'L0_attn_Wv': _L0_attn_in['Wv'], 'L0_attn_Wo': _L0_attn_in['Wo'], 'L0_ffn_gate_w': _L0_ffn_in['gate_w'], 'L0_ffn_expert_w': _L0_ffn_in['expert_w']}

def reference(x, txt, L0_tok_W_lin, L0_tok_b_lin, L0_tok_class_token, L0_tok_position_embeddings, L0_attn_Wq, L0_attn_Wk, L0_attn_Wv, L0_attn_Wo, L0_ffn_gate_w, L0_ffn_expert_w):
    import jax
    import jax.numpy as jnp

    def _L0_tok_ref(data, W_lin, b_lin, class_token, position_embeddings):
        import jax, jax.numpy as jnp
        import numpy as np
        B, C, H, W = (64, 3, 96, 96)
        P = 16
        HP, WP = (H // P, W // P)
        N = HP * WP
        F = C * P * P
        D = 256
        b = data.shape[0]
        x = data.reshape(b, C, HP, P, WP, P)
        x = x.transpose(0, 2, 4, 1, 3, 5).reshape(b, N, F)
        x = jnp.einsum('bnf,df->bnd', x, W_lin) + b_lin
        cls = jnp.broadcast_to(class_token, (b, 1, D))
        out = jnp.concatenate([cls, x], axis=1) + position_embeddings
        return out

    def _L0_attn_ref(hidden_states, Wq, Wk, Wv, Wo):
        import jax, jax.numpy as jnp
        import numpy as np
        WIN = 64
        STRIDE = 128
        HEADS = 16
        B, S, D = hidden_states.shape
        H = HEADS
        dh = D // H
        nw = (S - WIN) // STRIDE + 1
        idx = jnp.arange(nw)[:, None] * STRIDE + jnp.arange(WIN)[None, :]
        win = hidden_states[:, idx]

        def proj(x, Wm):
            return jnp.einsum('bnwd,de->bnwe', x, Wm).reshape(B, nw, WIN, H, dh)
        q = proj(win, Wq)
        k = proj(win, Wk)
        v = proj(win, Wv)
        scores = jnp.einsum('bnqhd,bnkhd->bnhqk', q, k) / jnp.sqrt(jnp.asarray(dh, q.dtype))
        attn = jax.nn.softmax(scores, axis=-1)
        ctx = jnp.einsum('bnhqk,bnkhd->bnqhd', attn, v)
        ctx = ctx.reshape(B, nw, WIN, D)
        win_out = jnp.einsum('bnwd,de->bnwe', ctx, Wo)
        flat_idx = idx.reshape(-1)
        out = jnp.zeros((B, S, D), hidden_states.dtype).at[:, flat_idx].add(win_out.reshape(B, nw * WIN, D))
        count = jnp.zeros((S,), hidden_states.dtype).at[flat_idx].add(1.0)
        out = out / (count[None, :, None] + 1e-08)
        return out

    def _L0_ffn_ref(x, gate_w, expert_w):
        import jax, jax.numpy as jnp
        import numpy as np
        NUM_EXPERTS = 8
        TOP_K = 2
        N_EMBD = 256
        B, T = (4, 512)
        Bb, Tt, C = x.shape
        xf = x.reshape(Bb * Tt, C)
        logits = xf @ gate_w.T
        w, sel = jax.lax.top_k(logits, TOP_K)
        w = jax.nn.softmax(w.astype(jnp.float32), axis=1).astype(xf.dtype)
        n = xf.shape[0]
        w_full = jnp.zeros((n, NUM_EXPERTS), dtype=xf.dtype)
        w_full = w_full.at[jnp.arange(n)[:, None], sel].add(w)
        expert_out = jnp.einsum('nc,edc->ned', xf, expert_w)
        out = jnp.einsum('ne,ned->nd', w_full, expert_out)
        return out.reshape(Bb, Tt, C)
    h = _L0_tok_ref(x, L0_tok_W_lin, L0_tok_b_lin, L0_tok_class_token, L0_tok_position_embeddings)
    h = jnp.concatenate([h, txt], axis=1)
    h = h + _L0_attn_ref(_layernorm(h, axis=-1), L0_attn_Wq, L0_attn_Wk, L0_attn_Wv, L0_attn_Wo)
    h = h + _L0_ffn_ref(_layernorm(h, axis=-1), L0_ffn_gate_w, L0_ffn_expert_w)
    return h

_drawn_inputs = setup_inputs


def setup_inputs(seed=0):
    import zlib

    import numpy as np

    out = dict(_drawn_inputs(seed))
    spreads = {}
    factors = {'L0_attn_Wq': 6.996, 'L0_attn_Wk': 8.0, 'L0_attn_Wv': 2.864}
    for name, (base, spread) in spreads.items():
        noise = np.random.default_rng([zlib.crc32(name.encode()), seed]).standard_normal(out[name].shape)
        drawn = base * np.exp(spread * noise) if base else spread * noise
        out[name] = jnp.asarray(drawn.astype(out[name].dtype))
    for name, factor in factors.items():
        out[name] = (out[name] * factor).astype(out[name].dtype)
    return out
```

```python
from contextlib import ExitStack

import concourse.bass as bass
from concourse import mybir

F32 = mybir.dt.float32
F32R = mybir.dt.float32r
F16 = mybir.dt.float16
BF16 = mybir.dt.bfloat16
U32 = mybir.dt.uint32
ALU = mybir.AluOpType
ACT = mybir.ActivationFunctionType
AX_X = mybir.AxisListType.X

P = 128
D = 256
KD = D // P
B = 32
S = 114
WIN = 64
NPATCH = 36
FEAT = 768
KF = FEAT // P
HEADS = 16
DH = D // HEADS
NE = 8
GB = 4
PAIRS = B // 2
NG = B // GB
NREST = B * (S - WIN)
RT = NREST // P
RLAST = NREST - RT * P
CH = NE * D // 512
TXT_WIN = WIN - NPATCH - 1
EPS = 1e-5


def fusion_kernel(nc, xT, wlinT, posT, blin, cls, txt_win, rest, rest_last, wq, wk, wv, wo,
                  gateT, expT, consts, out_win, out_rest, out_rest_last):
    ctx = ExitStack()
    with ctx:
        def sb(name, shape, dt=F32):
            return ctx.enter_context(nc.sbuf_tensor(name, shape, dt))

        def bank(name, shape):
            return ctx.enter_context(nc.psum_tensor(name, shape, F32))

        def sem(name):
            return ctx.enter_context(nc.semaphore(name))

        const = sb("const", [P, P + 4 + NE])
        ident = const[:, 0:P]
        head_mask = const[:, P:P + 4]
        iota_e = const[:, P + 4:P + 4 + NE]
        eps_col = sb("eps_col", [P, 3])
        wlin = sb("wlin", [P, KF, D])
        pos = sb("pos", [P, KD, NPATCH + 1])
        bias = sb("bias", [P, KD])
        clst = sb("clst", [P, KD])
        patch_add = sb("patch_add", [P, KD, NPATCH])
        w_raw = sb("w_raw", [P, 4, KD, D])
        w_hi = sb("w_hi", [P, 4, KD, D], F32R)
        w_lo = sb("w_lo", [P, 4, KD, D], F32R)
        g_raw = sb("g_raw", [P, KD, NE])
        g_hi = sb("g_hi", [P, KD, NE], F32R)
        g_lo = sb("g_lo", [P, KD, NE], F32R)
        e_raw = sb("e_raw", [P, KD, NE * D])
        e_hi = sb("e_hi", [P, KD, NE * D], F32R)
        e_lo = sb("e_lo", [P, KD, NE * D], F32R)

        win = sb("win", [P, PAIRS * D])
        rst = sb("rst", [P, (RT + 1) * D])

        xg = sb("xg", [P, KF, GB * NPATCH])
        hT = sb("hT", [P, KD, GB, WIN])
        norm1 = sb("norm1", [P, 2, D])
        x1_hi = sb("x1_hi", [P, KD, 2 * P], F32R)
        x1_lo = sb("x1_lo", [P, KD, 2 * P], F32R)
        q_bd = sb("q_bd", [P, KD, GB, 2, WIN])
        k_bd = sb("k_bd", [P, KD, GB, 4, WIN])
        v_bd = [sb(f"v_bd{n}", [P, 2 * 8, 2, 32], BF16) for n in range(3)]
        v_rest = sb("v_rest", [P, 2 * 8, 32])

        smax = sb("smax", [P, 16])
        s_sub = sb("s_sub", [P, 2, 8, WIN])
        prob = sb("prob", [P, 8, 2, WIN])
        ssum = sb("ssum", [P, 16])
        sinv = sb("sinv", [P, 16])
        pT_hi = sb("pT_hi", [P, 8, P], F16)
        pT_lo = sb("pT_lo", [P, 8, P], F16)
        attn = sb("attn", [P, 2, 8, DH])
        cT_hi = sb("cT_hi", [P, 2, 2, WIN], F32R)
        cT_lo = sb("cT_lo", [P, 2, 2, WIN], F32R)

        norm2 = sb("norm2", [P, 3, D])
        x2_hi = sb("x2_hi", [P, 3, KD, P], F32R)
        x2_lo = sb("x2_lo", [P, 3, KD, P], F32R)
        logit = sb("logit", [P, 3, NE])
        top8 = sb("top8", [P, 3, 8])
        topi = sb("topi", [P, 3, 8], U32)
        topf = sb("topf", [P, 3, 2])
        wexp = sb("wexp", [P, 3, 4])
        wsel = sb("wsel", [P, 3, 2, NE])
        wfull = sb("wfull", [P, 3, NE])

        bn = sb("bn", [P, 5, 6])
        mv = sb("mv", [P, 5, 2])
        ve = sb("ve", [P, 5])
        rstd = sb("rstd", [P, 5])

        SP_ = bank("score_bank", [P, 2, 512])
        O_ = bank("value_bank", [P, 8, 2, 2, DH])
        T_ = bank("norm_t_bank", [P, KD, P])
        U_ = bank("small_bank", [P, 512])
        PR = bank("proj_bank", [P, 512])
        XB = [bank(f"expert_bank{n}", [P, 512]) for n in range(2)]

        names = """d_const d_wlin d_embc d_x d_txt d_rest0 d_rest d_attw d_gate d_exp d_out
            zeroed consts_ready patch_const
            attw_hi attw_lo gate_hi gate_lo exp_hi exp_lo_a exp_lo_b
            emb_done emb_added hT_done win_added
            bn1 mv1 rstd1_ve rstd1 norm1_ready x1T_done x1_hi_done x1_lo_done
            q_done q_taken k_done k_taken v_done v1_taken vr_ready v2_ready v3_ready
            score_done max_done sub_done exp_done sum_done inv_done
            pT_done pT_hi_done pT_lo_done pv_done attn_ready cT_done cT_hi_done cT_lo_done
            wo_done res_done bnw mvw rstdw_ve rstdw
            bnr mvr rstdr_ve rstdr
            norm2_ready x2T_done x2_hi_done x2_lo_done
            logit_done top_val logit_taken index_done ex_done gi_done gd_done g0_done g1_done gm_done gs_done
            weights_ready chunk_done chunk_part chunk_used"""
        m = {n: sem(n) for n in names.split()}

        def wait(eng, name, value):
            if not (isinstance(value, int) and value <= 0):
                eng.wait_ge(m[name], value)

        def wait_apart(eng, name, value):
            if not isinstance(value, int):
                eng.wait_ge(m["consts_ready"], 1)
            wait(eng, name, value)

        def win_at(t):
            return win[:, bass.ds(t * D, D)]

        def rst_at(r, rows=P):
            return rst[0:rows, bass.ds(r * D, D)]

        def tile_no(s, slot):
            return 0 if isinstance(s, int) and s == 0 else 3 * s - 2 + slot

        X_EPI = 3 * (NG - 1) - 2 + 3
        R_FIRST = NG

        def first(s):
            return isinstance(s, int) and s == 0

        def last(s):
            return isinstance(s, int) and s == NG - 1

        def slots(s):
            return (0,) if first(s) else (0, 1, 2)

        block = ctx.enter_context(nc.Block())

        @block.sync
        def _(sp):
            sp.dma_start(const[:], consts).then_inc(m["d_const"], 16)
            sp.dma_start(xg[:], xT[0]).then_inc(m["d_x"], 16)
            sp.dma_start(wlin[:], wlinT).then_inc(m["d_wlin"], 16)
            sp.wait_ge(m["zeroed"], 1)
            for b in range(2):
                sp.dma_start(win[WIN * b + NPATCH + 1:WIN * (b + 1), :], txt_win[b]).then_inc(m["d_txt"], 16)
            sp.dma_start(e_raw[:], expT).then_inc(m["d_exp"], 16)
            sp.dma_start(rst[:, D:RT * D], rest[:, D:RT * D]).then_inc(m["d_rest"], 16)
            sp.dma_start(rst[0:RLAST, RT * D:(RT + 1) * D], rest_last).then_inc(m["d_rest"], 16)

            def load_patches(s):
                wait(sp, "emb_done", s + 2)
                sp.dma_start(xg[:], xT[s + 2] if isinstance(s, int) else
                             xT[bass.ds(s + 2, 1)].squeeze(0)).then_inc(m["d_x"], 16)

            def store_rest(x, r):
                wait(sp, "chunk_used", CH * (x + 1))
                sp.dma_start(out_rest[:, bass.ds(r * D, D)], rst_at(r)).then_inc(m["d_out"], 16)

            def store_win(x, t):
                wait(sp, "chunk_used", CH * (x + 1))
                sp.dma_start(out_win[:, bass.ds(t * D, D)], win_at(t)).then_inc(m["d_out"], 16)

            wait(sp, "emb_done", 1)
            sp.dma_start(xg[:], xT[1]).then_inc(m["d_x"], 16)

            def superstep(s, load=True):
                if load:
                    load_patches(s)
                store_rest(tile_no(s, 0), s)
                if not first(s):
                    store_win(tile_no(s, 1), 2 * s - 2)
                    store_win(tile_no(s, 2), 2 * s - 1)

            superstep(0)
            with sp.Fori(1, NG - 2) as s:
                superstep(s)
            superstep(NG - 2, load=False)
            superstep(NG - 1, load=False)
            store_win(X_EPI, PAIRS - 2)
            store_win(X_EPI + 1, PAIRS - 1)
            for r in range(R_FIRST, RT):
                store_rest(X_EPI + 2 + r - R_FIRST, r)
            wait(sp, "chunk_used", CH * (X_EPI + 3 + RT - R_FIRST))
            sp.dma_start(out_rest_last, rst_at(RT, RLAST)).then_inc(m["d_out"], 16)
            sp.wait_ge(m["d_out"], 16 * (PAIRS + RT + 1))

        @block.gpsimd
        def _(pool):
            pool.memset(win[:], 0.0).then_inc(m["zeroed"], 1)
            pool.memset(hT[:], 0.0).then_inc(m["zeroed"], 1)
            pool.memset(eps_col[:, 0:1], EPS)
            pool.memset(eps_col[:, 1:2], -0.5)
            pool.memset(eps_col[:, 2:3], 1.0).then_inc(m["consts_ready"], 1)
            pool.wait_ge(m["consts_ready"], 1)

            def inverse_deviation(kind, n, slot, rows=P):
                wait(pool, {"rstd1": "mv1", "rstdw": "mvw", "rstdr": "mvr"}[kind], n + 1)
                pool.tensor_tensor(ve[0:rows, slot:slot + 1], mv[0:rows, slot, 1:2], eps_col[0:rows, 0:1],
                                   ALU.add).then_inc(m[kind + "_ve"], 1)
                wait(pool, kind + "_ve", n + 1)
                pool.tensor_tensor(rstd[0:rows, slot:slot + 1], ve[0:rows, slot:slot + 1],
                                   eps_col[0:rows, 1:2], ALU.pow).then_inc(m[kind], 1)

            def gate(x, slot, rows=P):
                e, den, w0, w1 = (wexp[0:rows, slot, n:n + 1] for n in range(4))
                wait(pool, "ex_done", x + 1)
                pool.tensor_tensor(den, e, eps_col[0:rows, 2:3], ALU.add).then_inc(m["gd_done"], 1)
                wait_apart(pool, "index_done", x + 1)
                pool.tensor_copy(topf[0:rows, slot], topi[0:rows, slot, 0:2]).then_inc(m["gi_done"], 1)
                wait(pool, "g0_done", x + 1)
                pool.tensor_tensor(w1, e, w0, ALU.mult).then_inc(m["g1_done"], 1)
                wait_apart(pool, "g1_done", x + 1)
                wait(pool, "gi_done", x + 1)
                for n, w in enumerate((w0, w1)):
                    pool.tensor_scalar(wsel[0:rows, slot, n], iota_e[0:rows], topf[0:rows, slot, n:n + 1], w,
                                       ALU.is_equal, ALU.mult).then_inc(m["gm_done"], 1)
                wait(pool, "gm_done", 2 * (x + 1))
                pool.tensor_tensor(wfull[0:rows, slot], wsel[0:rows, slot, 0], wsel[0:rows, slot, 1],
                                   ALU.add).then_inc(m["weights_ready"], 1)

            def last_v_part(g, before, count):
                wait(pool, before, count)
                wait(pool, "v2_ready", 2 * (g + 1))
                wait(pool, "vr_ready", 2 * (g + 1))
                for b in range(2):
                    h = slice(WIN * b, WIN * (b + 1))
                    pool.tensor_tensor(v_bd[2][h, :, b], v_rest[h], v_bd[1][h, :, b],
                                       ALU.subtract).then_inc(m["v3_ready"], 1)
                    wait(pool, "v3_ready", 2 * g + b + 1)

            pool.wait_ge(m["d_const"], 16)
            inverse_deviation("rstdr", 0, 4)
            inverse_deviation("rstd1", 0, 0)
            inverse_deviation("rstd1", 1, 1)
            pool.wait_ge(m["exp_hi"], 2)
            for n in range(4):
                c = slice(n * 512, (n + 1) * 512)
                pool.tensor_tensor(e_lo[:, 1, c], e_raw[:, 1, c], e_hi[:, 1, c].bitcast(F32),
                                   ALU.subtract).then_inc(m["exp_lo_b"], 1)
            pool.wait_ge(m["patch_const"], 1)
            last_v_part(0, "exp_lo_b", 4)

            def superstep(s):
                gate(tile_no(s, 0), 0)
                if not last(s):
                    inverse_deviation("rstd1", 2 * (s + 1), 0)
                    inverse_deviation("rstd1", 2 * (s + 1) + 1, 1)
                if not first(s):
                    gate(tile_no(s, 1), 1)
                inverse_deviation("rstdw", 2 * s, 2)
                if not first(s):
                    gate(tile_no(s, 2), 2)
                if not last(s):
                    if first(s):
                        last_v_part(1, "rstdw", 1)
                    else:
                        last_v_part(s + 1, "weights_ready", tile_no(s, 2) + 1)
                inverse_deviation("rstdw", 2 * s + 1, 3)
                inverse_deviation("rstdr", s + 1, 4)

            superstep(0)
            with pool.Fori(1, NG - 1) as s:
                superstep(s)
            superstep(NG - 1)
            gate(X_EPI, 1)
            gate(X_EPI + 1, 2)
            for r in range(R_FIRST, RT + 1):
                rows = P if r < RT else RLAST
                x = X_EPI + 2 + r - R_FIRST
                if r + 1 <= RT:
                    inverse_deviation("rstdr", r + 1, 4, P if r + 1 < RT else RLAST)
                gate(x, (r - R_FIRST) % 3, rows)

        @block.scalar
        def _(act):
            act.dma_start(rst[:, 0:D], rest[:, 0:D]).then_inc(m["d_rest0"], 16)
            act.dma_start(pos[:], posT).then_inc(m["d_embc"], 16)
            act.dma_start(bias[:], blin).then_inc(m["d_embc"], 16)
            act.dma_start(clst[:], cls).then_inc(m["d_embc"], 16)
            for n, w in enumerate((wq, wk, wv, wo)):
                act.dma_start(w_raw[:, n], w).then_inc(m["d_attw"], 16)
            act.dma_start(g_raw[:], gateT).then_inc(m["d_gate"], 16)

            def copy(out, in_, **kw):
                return act.activation(out, in_, ACT.Copy, **kw)

            def norm2_hi(x, slot, rows=P):
                wait(act, "x2T_done", x + 1)
                copy(x2_hi[:, slot, :, 0:rows], T_[:, :, 0:rows]).then_inc(m["x2_hi_done"], 1)

            def gate_exp(x, slot, rows=P):
                wait(act, "top_val", x + 1)
                act.activation(wexp[0:rows, slot, 0:1], top8[0:rows, slot, 0:1], ACT.Exp, scale=-1.0,
                               bias=top8[0:rows, slot, 1:2]).then_inc(m["ex_done"], 1)

            def softmax_exp(t):
                wait(act, "sub_done", t + 1)
                act.activation(prob[:].rearrange("p c b k -> p b c k"), s_sub[:], ACT.Exp).then_inc(m["exp_done"], 1)

            def prob_hi(t):
                wait(act, "pT_done", t + 1)
                copy(pT_hi[:].rearrange("p c q -> p (c q)"),
                     SP_[:].rearrange("p b n -> p (b n)")).then_inc(m["pT_hi_done"], 1)

            def context_hi(t):
                wait(act, "cT_done", t + 1)
                copy(cT_hi[:].rearrange("p h b q -> p b h q"),
                     U_[:, 0:D].rearrange("p (b h q) -> p b h q", b=2, h=2)).then_inc(m["cT_hi_done"], 1)

            def norm1_hi(g, j):
                wait(act, "x1T_done", 2 * g + j + 1)
                copy(x1_hi[:, :, P * j:P * (j + 1)], T_[:]).then_inc(m["x1_hi_done"], 1)

            def take_q(g):
                wait(act, "q_done", g + 1)
                if first(g):
                    act.wait_ge(m["patch_const"], 1)
                src = PR[:].rearrange("p (n q) -> p n q", q=WIN)
                for hs in range(2):
                    h = slice(WIN * hs, WIN * (hs + 1))
                    copy(q_bd[h].rearrange("p c b h q -> p (c b) h q")[:, :, hs], src[h],
                         scale=DH ** -0.5).then_inc(m["q_taken"], 1)

            def take_k(g):
                wait(act, "k_done", g + 1)
                src = PR[:].rearrange("p (n q) -> p n q", q=WIN)
                for hh in range(4):
                    copy(k_bd[:].rearrange("p c b h k -> p (c b) h k")[:, :, hh], src,
                         scale=head_mask[:, hh:hh + 1]).then_inc(m["k_taken"], 1)

            def take_v(g):
                wait(act, "v_done", g + 1)
                src = PR[:].rearrange("p (n d) -> p n d", d=32)
                for b in range(2):
                    h = slice(WIN * b, WIN * (b + 1))
                    copy(v_bd[0][h, :, b], src[h]).then_inc(m["v1_taken"], 1)

            def second_v_part(g):
                wait(act, "vr_ready", 2 * (g + 1))
                for b in range(2):
                    h = slice(WIN * b, WIN * (b + 1))
                    copy(v_bd[1][h, :, b], v_rest[h]).then_inc(m["v2_ready"], 1)

            act.wait_ge(m["d_attw"], 64)
            act.wait_ge(m["d_const"], 16)
            copy(w_hi[:].rearrange("p a b c -> p (a b c)"),
                 w_raw[:].rearrange("p a b c -> p (a b c)")).then_inc(m["attw_hi"], 1)
            act.wait_ge(m["d_gate"], 16)
            copy(g_hi[:], g_raw[:]).then_inc(m["gate_hi"], 1)
            norm2_hi(0, 0)
            norm1_hi(0, 0)
            norm1_hi(0, 1)
            act.wait_ge(m["d_exp"], 16)
            for k in range(KD):
                copy(e_hi[:, k], e_raw[:, k]).then_inc(m["exp_hi"], 1)
            take_q(0)
            take_k(0)
            take_v(0)
            second_v_part(0)

            def superstep(s):
                softmax_exp(2 * s)
                gate_exp(tile_no(s, 0), 0)
                prob_hi(2 * s)
                if not first(s):
                    norm2_hi(tile_no(s, 1), 1)
                if not first(s):
                    gate_exp(tile_no(s, 1), 1)
                softmax_exp(2 * s + 1)
                context_hi(2 * s)
                if not last(s):
                    norm1_hi(s + 1, 0)
                    norm1_hi(s + 1, 1)
                prob_hi(2 * s + 1)
                if not last(s):
                    take_q(s + 1)
                if not first(s):
                    norm2_hi(tile_no(s, 2), 2)
                if not last(s):
                    take_k(s + 1)
                if not first(s):
                    gate_exp(tile_no(s, 2), 2)
                context_hi(2 * s + 1)
                if not last(s):
                    take_v(s + 1)
                    second_v_part(s + 1)
                    norm2_hi(tile_no(s, 0) + len(slots(s)), 0)

            superstep(0)
            with act.Fori(1, NG - 1) as s:
                superstep(s)
            superstep(NG - 1)
            norm2_hi(X_EPI, 1)
            gate_exp(X_EPI, 1)
            norm2_hi(X_EPI + 1, 2)
            gate_exp(X_EPI + 1, 2)
            for r in range(R_FIRST, RT + 1):
                rows = P if r < RT else RLAST
                norm2_hi(X_EPI + 2 + r - R_FIRST, (r - R_FIRST) % 3, rows)
                gate_exp(X_EPI + 2 + r - R_FIRST, (r - R_FIRST) % 3, rows)

        @block.vector
        def _(dve):
            def stats(kind, n, slot, src, rows=P):
                bn_sem, mv_sem = {"1": ("bn1", "mv1"), "w": ("bnw", "mvw"), "r": ("bnr", "mvr")}[kind]
                dve.bn_stats(bn[0:rows, slot], src).then_inc(m[bn_sem], 1)
                wait_apart(dve, bn_sem, n + 1)
                dve.bn_aggr(mv[0:rows, slot], bn[0:rows, slot]).then_inc(m[mv_sem], 1)

            def normalise(out, src, slot, rows=P):
                return dve.tensor_scalar(out, src, mv[0:rows, slot, 0:1], rstd[0:rows, slot:slot + 1],
                                         ALU.subtract, ALU.mult)

            def norm2_win(x, slot, t):
                wait(dve, "rstdw", t + 1)
                normalise(norm2[:, slot], win_at(t), 1 + slot).then_inc(m["norm2_ready"], 1)

            def norm2_rest(x, slot, r, rows=P):
                wait(dve, "rstdr", r + 1)
                normalise(norm2[0:rows, slot], rst_at(r, rows), 4, rows).then_inc(m["norm2_ready"], 1)

            def norm2_lo(x, slot, rows=P):
                wait(dve, "x2_hi_done", x + 1)
                dve.tensor_tensor(x2_lo[:, slot, :, 0:rows], T_[:, :, 0:rows],
                                  x2_hi[:, slot, :, 0:rows].bitcast(F32), ALU.subtract).then_inc(m["x2_lo_done"], 1)

            def top_two(x, slot, rows=P):
                wait(dve, "logit_done", x + 1)
                lg = logit[0:rows, slot]
                dve.tensor_copy(lg, U_[0:rows, 0:NE]).then_inc(m["logit_taken"], 1)
                wait_apart(dve, "logit_taken", x + 1)
                dve.max(top8[0:rows, slot], lg).then_inc(m["top_val"], 1)
                wait_apart(dve, "top_val", x + 1)
                dve.max_index(topi[0:rows, slot], top8[0:rows, slot], lg).then_inc(m["index_done"], 1)

            def first_weight(x, slot, rows=P):
                wait(dve, "gd_done", x + 1)
                dve.reciprocal(wexp[0:rows, slot, 2:3], wexp[0:rows, slot, 1:2]).then_inc(m["g0_done"], 1)

            def experts(x, slot, c, acc, rows=P):
                if c == 0:
                    wait(dve, "weights_ready", x + 1)
                wait(dve, "chunk_done", CH * x + c + 1)
                for n in range(2):
                    e = 2 * c + n
                    i = dve.scalar_tensor_tensor(out=acc, in0=XB[c % 2][0:rows, D * n:D * (n + 1)],
                                                 scalar=wfull[0:rows, slot, e:e + 1], in1=acc,
                                                 op0=ALU.mult, op1=ALU.add)
                    if n == 0:
                        i.then_inc(m["chunk_part"], 1)
                        wait(dve, "chunk_part", CH * x + c + 1)
                i.then_inc(m["chunk_used"], 1)
                if c < CH - 1:
                    wait(dve, "chunk_used", CH * x + c + 1)

            def take_embedding(g):
                wait(dve, "emb_done", g + 1)
                src = PR[:, 0:KD * GB * NPATCH].rearrange("p (c b n) -> p c b n", c=KD, b=GB)
                dve.tensor_tensor(hT[:, :, :, 0:NPATCH], src,
                                  patch_add[:].unsqueeze(2).to_broadcast([P, KD, GB, NPATCH]),
                                  ALU.add).then_inc(m["emb_added"], 1)

            def add_window(g, j):
                t = 2 * g + j
                wait(dve, "hT_done", t + 1)
                dve.tensor_tensor(win_at(t), U_[:, 0:D], win_at(t), ALU.add).then_inc(m["win_added"], 1)
                wait_apart(dve, "win_added", t + 1)
                stats("1", t, j, win_at(t))

            def norm1_window(g, j):
                wait(dve, "rstd1", 2 * g + j + 1)
                normalise(norm1[:, j], win_at(2 * g + j), j).then_inc(m["norm1_ready"], 1)

            def norm1_lo(g, j):
                wait(dve, "x1_hi_done", 2 * g + j + 1)
                c = slice(P * j, P * (j + 1))
                dve.tensor_tensor(x1_lo[:, :, c], T_[:], x1_hi[:, :, c].bitcast(F32),
                                  ALU.subtract).then_inc(m["x1_lo_done"], 1)

            def softmax_max(t):
                wait(dve, "score_done", t + 1)
                s = SP_[:].rearrange("p b (c k) -> p (b c) k", k=WIN)
                dve.reduce_max(smax[:], s, AX_X).then_inc(m["max_done"], 1)
                wait(dve, "max_done", t + 1)
                dve.tensor_tensor(s_sub[:].rearrange("p b c k -> p (b c) k"), s,
                                  smax[:].unsqueeze(2).to_broadcast([P, 16, WIN]),
                                  ALU.subtract).then_inc(m["sub_done"], 1)

            def softmax_sum(t):
                wait(dve, "exp_done", t + 1)
                dve.reduce_sum(ssum[:], prob[:].rearrange("p c b k -> p (c b) k"), AX_X).then_inc(m["sum_done"], 1)
                wait(dve, "sum_done", t + 1)
                dve.reciprocal(sinv[:], ssum[:]).then_inc(m["inv_done"], 1)

            def prob_lo(t):
                wait(dve, "pT_hi_done", t + 1)
                dve.tensor_tensor(pT_lo[:].rearrange("p c q -> p (c q)"), SP_[:].rearrange("p b n -> p (b n)"),
                                  pT_hi[:].rearrange("p c q -> p (c q)"), ALU.subtract).then_inc(m["pT_lo_done"], 1)

            def take_context(t):
                wait(dve, "pv_done", t + 1)
                wait(dve, "inv_done", t + 1)
                for hs in range(2):
                    h = slice(WIN * hs, WIN * (hs + 1))
                    dve.tensor_tensor(attn[h].rearrange("p b c d -> p c b d"), O_[h, :, :, hs],
                                      sinv[h].rearrange("p (c b) -> p c b", b=2).unsqueeze(3)
                                      .to_broadcast([WIN, 8, 2, DH]), ALU.mult).then_inc(m["attn_ready"], 1)

            def context_lo(t):
                wait(dve, "cT_hi_done", t + 1)
                dve.tensor_tensor(cT_lo[:].rearrange("p h b q -> p b h q"),
                                  U_[:, 0:D].rearrange("p (b h q) -> p b h q", b=2, h=2),
                                  cT_hi[:].rearrange("p h b q -> p b h q").bitcast(F32),
                                  ALU.subtract).then_inc(m["cT_lo_done"], 1)

            def add_attention(s, j):
                t = 2 * s + j
                wait(dve, "wo_done", t + 1)
                dve.tensor_tensor(win_at(t), U_[:, 0:D], win_at(t), ALU.add).then_inc(m["res_done"], 1)
                wait_apart(dve, "res_done", t + 1)
                stats("w", t, 2 + j, win_at(t))

            def v_minus_first(g):
                wait(dve, "v1_taken", 2 * (g + 1))
                src = PR[:].rearrange("p (n d) -> p n d", d=32)
                for b in range(2):
                    h = slice(WIN * b, WIN * (b + 1))
                    dve.tensor_tensor(v_rest[h], src[h], v_bd[0][h, :, b], ALU.subtract).then_inc(m["vr_ready"], 1)

            dve.memset(q_bd[:], 0.0)
            for n in range(3):
                dve.memset(v_bd[n][:], 0.0)
            dve.wait_ge(m["d_embc"], 48)
            for c in range(KD):
                dve.tensor_scalar(patch_add[:, c], pos[:, c, 1:NPATCH + 1], bias[:, c:c + 1], None, ALU.add)
            dve.wait_ge(m["zeroed"], 2)
            dve.tensor_tensor(hT[:, :, :, NPATCH:NPATCH + 1],
                              pos[:, :, 0:1].unsqueeze(2).to_broadcast([P, KD, GB, 1]),
                              clst[:].unsqueeze(2).unsqueeze(3).to_broadcast([P, KD, GB, 1]),
                              ALU.add).then_inc(m["patch_const"], 1)
            dve.wait_ge(m["d_rest0"], 16)
            stats("r", 0, 4, rst_at(0))
            dve.wait_ge(m["patch_const"], 1)
            norm2_rest(0, 0, 0)
            dve.wait_ge(m["attw_hi"], 1)
            dve.tensor_tensor(w_lo[:].rearrange("p a b c -> p (a b c)"), w_raw[:].rearrange("p a b c -> p (a b c)"),
                              w_hi[:].rearrange("p a b c -> p (a b c)").bitcast(F32),
                              ALU.subtract).then_inc(m["attw_lo"], 1)
            dve.wait_ge(m["gate_hi"], 1)
            dve.tensor_tensor(g_lo[:], g_raw[:], g_hi[:].bitcast(F32), ALU.subtract).then_inc(m["gate_lo"], 1)
            norm2_lo(0, 0)
            take_embedding(0)
            dve.wait_ge(m["d_txt"], 32)
            for j in range(2):
                add_window(0, j)
            for j in range(2):
                norm1_window(0, j)
            for j in range(2):
                norm1_lo(0, j)
            dve.wait_ge(m["exp_hi"], 1)
            dve.tensor_tensor(e_lo[:, 0], e_raw[:, 0], e_hi[:, 0].bitcast(F32),
                              ALU.subtract).then_inc(m["exp_lo_a"], 1)
            v_minus_first(0)
            dve.wait_ge(m["d_rest"], 32)

            def superstep(s):
                x = [tile_no(s, n) for n in range(3)]
                accs = [rst_at(s), None, None] if first(s) else [rst_at(s), win_at(2 * s - 2), win_at(2 * s - 1)]
                softmax_max(2 * s)
                if not last(s):
                    take_embedding(s + 1)
                top_two(x[0], 0)
                if not first(s):
                    norm2_win(x[1], 1, 2 * s - 2)
                softmax_sum(2 * s)
                first_weight(x[0], 0)
                experts(x[0], 0, 0, accs[0])
                experts(x[0], 0, 1, accs[0])
                prob_lo(2 * s)
                if not first(s):
                    norm2_lo(x[1], 1)
                experts(x[0], 0, 2, accs[0])
                experts(x[0], 0, 3, accs[0])
                if not last(s):
                    for j in range(2):
                        add_window(s + 1, j)
                    for j in range(2):
                        norm1_window(s + 1, j)
                take_context(2 * s)
                if not first(s):
                    top_two(x[1], 1)
                    first_weight(x[1], 1)
                    experts(x[1], 1, 0, accs[1])
                softmax_max(2 * s + 1)
                if not first(s):
                    experts(x[1], 1, 1, accs[1])
                context_lo(2 * s)
                if not last(s):
                    norm1_lo(s + 1, 0)
                if not first(s):
                    experts(x[1], 1, 2, accs[1])
                add_attention(s, 0)
                if not last(s):
                    norm1_lo(s + 1, 1)
                if not first(s):
                    experts(x[1], 1, 3, accs[1])
                softmax_sum(2 * s + 1)
                if not first(s):
                    norm2_win(x[2], 2, 2 * s - 1)
                prob_lo(2 * s + 1)
                if not first(s):
                    norm2_lo(x[2], 2)
                take_context(2 * s + 1)
                if not first(s):
                    top_two(x[2], 2)
                    first_weight(x[2], 2)
                    experts(x[2], 2, 0, accs[2])
                    experts(x[2], 2, 1, accs[2])
                context_lo(2 * s + 1)
                if not last(s):
                    v_minus_first(s + 1)
                if not first(s):
                    experts(x[2], 2, 2, accs[2])
                add_attention(s, 1)
                stats("r", s + 1, 4, rst_at(s + 1))
                if not last(s):
                    norm2_rest(x[0] + len(slots(s)), 0, s + 1)
                if not first(s):
                    experts(x[2], 2, 3, accs[2])
                if not last(s):
                    norm2_lo(x[0] + len(slots(s)), 0)

            superstep(0)
            with dve.Fori(1, NG - 1) as s:
                superstep(s)
            superstep(NG - 1)
            norm2_win(X_EPI, 1, PAIRS - 2)
            norm2_lo(X_EPI, 1)
            for j in range(2):
                acc = win_at(PAIRS - 2 + j)
                top_two(X_EPI + j, 1 + j)
                first_weight(X_EPI + j, 1 + j)
                experts(X_EPI + j, 1 + j, 0, acc)
                if j == 0:
                    norm2_win(X_EPI + 1, 2, PAIRS - 1)
                else:
                    norm2_rest(X_EPI + 2, 0, R_FIRST)
                experts(X_EPI + j, 1 + j, 1, acc)
                norm2_lo(X_EPI + 1 + j, 2 if j == 0 else 0)
                experts(X_EPI + j, 1 + j, 2, acc)
                experts(X_EPI + j, 1 + j, 3, acc)
            for r in range(R_FIRST, RT + 1):
                x = X_EPI + 2 + r - R_FIRST
                rows = P if r < RT else RLAST
                nrows = P if r + 1 < RT else RLAST
                acc = rst_at(r, rows)
                if r < RT:
                    stats("r", r + 1, 4, rst_at(r + 1, nrows), nrows)
                top_two(x, (r - R_FIRST) % 3, rows)
                first_weight(x, (r - R_FIRST) % 3, rows)
                experts(x, (r - R_FIRST) % 3, 0, acc, rows)
                if r < RT:
                    norm2_rest(x + 1, (r + 1 - R_FIRST) % 3, r + 1, nrows)
                experts(x, (r - R_FIRST) % 3, 1, acc, rows)
                if r < RT:
                    norm2_lo(x + 1, (r + 1 - R_FIRST) % 3, nrows)
                experts(x, (r - R_FIRST) % 3, 2, acc, rows)
                experts(x, (r - R_FIRST) % 3, 3, acc, rows)

        @block.tensor
        def _(pe):
            def split_product(out, terms, count=None):
                n = 0
                for (lh, ll), (rh, rl) in terms:
                    for lhs, rhs in ((lh, rh), (lh, rl), (ll, rh)):
                        n += 1
                        i = pe.matmul(out, lhs, rhs, start=(n == 1), stop=(n == 3 * len(terms)))
                return i

            def transpose_norm2(x, slot, rows=P):
                wait(pe, "norm2_ready", x + 1)
                for k in range(KD):
                    i = pe.transpose(T_[:, k, 0:rows], norm2[0:rows, slot, P * k:P * (k + 1)],
                                     ident[0:rows, 0:rows])
                i.then_inc(m["x2T_done"], 1)

            def x2(slot, k, rows):
                return x2_hi[:, slot, k, 0:rows], x2_lo[:, slot, k, 0:rows]

            def logits(x, slot, rows=P):
                wait(pe, "x2_lo_done", x + 1)
                split_product(U_[0:rows, 0:NE], [(x2(slot, k, rows), (g_hi[:, k], g_lo[:, k])) for k in range(KD)]
                              ).then_inc(m["logit_done"], 1)

            def experts(x, slot, c, rows=P):
                wait(pe, "chunk_used", CH * x + c - 1)
                w = slice(512 * c, 512 * (c + 1))
                split_product(XB[c % 2][0:rows], [(x2(slot, k, rows), (e_hi[:, k, w], e_lo[:, k, w]))
                                                  for k in range(KD)]).then_inc(m["chunk_done"], 1)

            def embed(g):
                wait(pe, "d_x", 16 * (g + 1))
                for c in range(KD):
                    for k in range(KF):
                        i = pe.matmul(PR[:, GB * NPATCH * c:GB * NPATCH * (c + 1)], wlin[:, k, P * c:P * (c + 1)],
                                      xg[:, k], start=(k == 0), stop=(k == KF - 1))
                i.then_inc(m["emb_done"], 1)

            def embed_back(g, j):
                wait(pe, "emb_added", g + 1)
                for c in range(KD):
                    i = pe.transpose(U_[:, P * c:P * (c + 1)],
                                     hT[:, c, 2 * j:2 * j + 2].rearrange("p b n -> p (b n)"), ident)
                i.then_inc(m["hT_done"], 1)

            def transpose_norm1(g, j):
                wait(pe, "norm1_ready", 2 * g + j + 1)
                for k in range(KD):
                    i = pe.transpose(T_[:, k], norm1[:, j, P * k:P * (k + 1)], ident)
                i.then_inc(m["x1T_done"], 1)

            def w_pair(n, k, cols):
                return w_hi[:, n, k, cols], w_lo[:, n, k, cols]

            def project(g, n, name):
                for c in range(KD):
                    i = split_product(PR[:, 2 * P * c:2 * P * (c + 1)],
                                      [(w_pair(n, k, slice(P * c, P * (c + 1))), (x1_hi[:, k], x1_lo[:, k]))
                                       for k in range(KD)])
                i.then_inc(m[name], 1)

            def project_v(g):
                for j in range(2):
                    c = slice(P * j, P * (j + 1))
                    i = split_product(PR[:, D * j:D * (j + 1)],
                                      [((x1_hi[:, k, c], x1_lo[:, k, c]), w_pair(2, k, slice(0, D)))
                                       for k in range(KD)])
                i.then_inc(m["v_done"], 1)

            def scores(s, j):
                t = 2 * s + j
                wait(pe, "q_taken", 2 * (s + 1))
                wait(pe, "k_taken", 4 * (s + 1))
                wait(pe, "pT_lo_done", t)
                for b in range(2):
                    for c in range(KD):
                        i = pe.matmul(SP_[:, b, D * c:D * (c + 1)],
                                      q_bd[:, c, 2 * j + b].rearrange("p h q -> p (h q)"),
                                      k_bd[:, c, 2 * j + b].rearrange("p h k -> p (h k)"), start=True, stop=True)
                i.then_inc(m["score_done"], 1)

            def transpose_prob(t):
                wait(pe, "exp_done", t + 1)
                pt = SP_[:].rearrange("p b (c q) -> p (b c) q", q=P)
                for c in range(8):
                    i = pe.transpose(pt[:, c], prob[:, c].rearrange("p b k -> p (b k)"), ident)
                i.then_inc(m["pT_done"], 1)

            def values(s, j):
                t = 2 * s + j
                wait(pe, "pT_lo_done", t + 1)
                wait(pe, "v3_ready", 2 * (s + 1))
                wait(pe, "attn_ready", 2 * t)
                for c in range(8):
                    terms = [(pT_hi, 0), (pT_hi, 1), (pT_hi, 2), (pT_lo, 0), (pT_lo, 1)]
                    for n, (pr, v) in enumerate(terms):
                        i = pe.matmul(O_[:, c].rearrange("p b h d -> p (b h d)"), pr[:, c],
                                      v_bd[v][:, 8 * j + c].rearrange("p b d -> p (b d)"),
                                      start=(n == 0), stop=(n == len(terms) - 1))
                i.then_inc(m["pv_done"], 1)

            def transpose_context(t):
                wait(pe, "attn_ready", 2 * (t + 1))
                for b in range(2):
                    i = pe.transpose(U_[:, P * b:P * (b + 1)], attn[:, b].rearrange("p c d -> p (c d)"), ident)
                i.then_inc(m["cT_done"], 1)

            def project_out(t):
                wait(pe, "cT_lo_done", t + 1)
                split_product(U_[:, 0:D],
                              [((cT_hi[:, h].rearrange("p b q -> p (b q)"), cT_lo[:, h].rearrange("p b q -> p (b q)")),
                                w_pair(3, h, slice(0, D))) for h in range(2)]).then_inc(m["wo_done"], 1)

            pe.wait_ge(m["d_const"], 16)
            transpose_norm2(0, 0)
            pe.wait_ge(m["d_wlin"], 16)
            embed(0)
            for j in range(2):
                wait(pe, "win_added", j)
                embed_back(0, j)
            wait(pe, "x2_lo_done", 1)
            transpose_norm1(0, 0)
            wait(pe, "x1_lo_done", 1)
            transpose_norm1(0, 1)
            wait(pe, "x1_lo_done", 2)
            pe.wait_ge(m["attw_lo"], 1)
            project(0, 0, "q_done")
            wait(pe, "q_taken", 2)
            project(0, 1, "k_done")
            wait(pe, "k_taken", 4)
            project_v(0)
            pe.wait_ge(m["gate_lo"], 1)

            def superstep(s):
                x = [tile_no(s, n) for n in range(3)]
                g = s + 1
                scores(s, 0)
                if not last(s):
                    wait(pe, "vr_ready", 2 * g)
                    embed(g)
                wait(pe, "res_done", 2 * s)
                if first(s):
                    wait(pe, "win_added", 2)
                logits(x[0], 0)
                if first(s):
                    pe.wait_ge(m["exp_lo_a"], 1)
                    pe.wait_ge(m["exp_lo_b"], 4)
                experts(x[0], 0, 0)
                experts(x[0], 0, 1)
                transpose_prob(2 * s)
                if not first(s):
                    transpose_norm2(x[1], 1)
                experts(x[0], 0, 2)
                experts(x[0], 0, 3)
                wait(pe, "logit_taken", x[0] + 1)
                if not last(s):
                    embed_back(g, 0)
                    wait(pe, "win_added", 2 * g + 1)
                    embed_back(g, 1)
                values(s, 0)
                if not last(s):
                    wait(pe, "win_added", 2 * g + 2)
                if not first(s):
                    logits(x[1], 1)
                    experts(x[1], 1, 0)
                scores(s, 1)
                if not first(s):
                    experts(x[1], 1, 1)
                    wait(pe, "logit_taken", x[1] + 1)
                transpose_context(2 * s)
                if not last(s):
                    if not first(s):
                        wait(pe, "x2_lo_done", x[1] + 1)
                    transpose_norm1(g, 0)
                if not first(s):
                    experts(x[1], 1, 2)
                project_out(2 * s)
                if not last(s):
                    wait(pe, "x1_lo_done", 2 * g + 1)
                    transpose_norm1(g, 1)
                if not first(s):
                    experts(x[1], 1, 3)
                transpose_prob(2 * s + 1)
                if not last(s):
                    wait(pe, "x1_lo_done", 2 * g + 2)
                    project(g, 0, "q_done")
                if not first(s):
                    transpose_norm2(x[2], 2)
                values(s, 1)
                if not last(s):
                    wait(pe, "q_taken", 2 * (g + 1))
                    project(g, 1, "k_done")
                wait(pe, "res_done", 2 * s + 1)
                if not first(s):
                    logits(x[2], 2)
                    experts(x[2], 2, 0)
                    experts(x[2], 2, 1)
                    wait(pe, "logit_taken", x[2] + 1)
                transpose_context(2 * s + 1)
                if not last(s):
                    wait(pe, "k_taken", 4 * (g + 1))
                    project_v(g)
                if not first(s):
                    experts(x[2], 2, 2)
                project_out(2 * s + 1)
                if not last(s):
                    if not first(s):
                        wait(pe, "x2_lo_done", x[2] + 1)
                    transpose_norm2(x[0] + len(slots(s)), 0)
                if not first(s):
                    experts(x[2], 2, 3)

            superstep(0)
            with pe.Fori(1, NG - 1) as s:
                superstep(s)
            superstep(NG - 1)
            wait(pe, "x2_lo_done", X_EPI)
            transpose_norm2(X_EPI, 1)
            tiles = [(1, P), (2, P)] + [((r - R_FIRST) % 3, P) for r in range(R_FIRST, RT)] + [((RT - R_FIRST) % 3, RLAST)]
            for n, (slot, rows) in enumerate(tiles):
                x = X_EPI + n
                wait(pe, "res_done", PAIRS)
                wait(pe, "logit_taken", x)
                logits(x, slot, rows)
                experts(x, slot, 0, rows)
                if n + 1 < len(tiles):
                    transpose_norm2(x + 1, *tiles[n + 1])
                for c in range(1, CH):
                    experts(x, slot, c, rows)


def kernel(x, txt, L0_tok_W_lin, L0_tok_b_lin, L0_tok_class_token, L0_tok_position_embeddings,
           L0_attn_Wq, L0_attn_Wk, L0_attn_Wv, L0_attn_Wo, L0_ffn_gate_w, L0_ffn_expert_w):
    import numpy as np
    import concourse.bacc as bacc
    from concourse.bass_utils import run_bass_kernel_spmd

    def chunks(a):
        a = np.asarray(a)
        return np.ascontiguousarray(a.reshape(-1, P, a.shape[-1]).transpose(1, 0, 2))

    x, txt = np.asarray(x), np.asarray(txt)
    xT = x.reshape(NG, GB, 3, 6, 16, 6, 16).transpose(0, 2, 4, 6, 1, 3, 5).reshape(NG, KF, P, GB * NPATCH)
    pos = np.asarray(L0_tok_position_embeddings)[0]
    text_in = txt[:, :TXT_WIN].reshape(PAIRS, 2, TXT_WIN, D).transpose(1, 2, 0, 3).reshape(2, TXT_WIN, PAIRS * D)
    rest = txt[:, TXT_WIN:].reshape(NREST, D)
    wv = np.asarray(L0_attn_Wv).reshape(D, 2, 2, 4, DH).transpose(0, 1, 3, 2, 4).reshape(D, D)
    wo = np.asarray(L0_attn_Wo).reshape(2, 2, 4, DH, D).transpose(1, 0, 2, 3, 4).reshape(D, D)
    heads = (np.arange(P)[:, None] % WIN // DH == np.arange(4)[None]).astype(np.float32)
    consts = np.concatenate([np.eye(P, dtype=np.float32), heads,
                             np.tile(np.arange(NE, dtype=np.float32), (P, 1))], axis=1)
    ins = {
        "xT": np.ascontiguousarray(xT.transpose(0, 2, 1, 3)),
        "wlinT": chunks(np.asarray(L0_tok_W_lin).T),
        "posT": chunks(pos.T),
        "blin": np.ascontiguousarray(np.asarray(L0_tok_b_lin).reshape(KD, P).T),
        "cls": np.ascontiguousarray(np.asarray(L0_tok_class_token).reshape(KD, P).T),
        "txt_win": np.ascontiguousarray(text_in),
        "rest": np.ascontiguousarray(rest[:RT * P].reshape(RT, P, D).transpose(1, 0, 2).reshape(P, RT * D)),
        "rest_last": np.ascontiguousarray(rest[RT * P:]),
        "wq": chunks(L0_attn_Wq), "wk": chunks(L0_attn_Wk), "wv": chunks(wv), "wo": chunks(wo),
        "gateT": chunks(np.asarray(L0_ffn_gate_w).T),
        "expT": chunks(np.asarray(L0_ffn_expert_w).transpose(2, 0, 1).reshape(D, NE * D)),
        "consts": consts,
    }
    outs = {"out_win": (P, PAIRS * D), "out_rest": (P, RT * D), "out_rest_last": (RLAST, D)}
    nc = bacc.Bacc("TRN2", target_bir_lowering=False, num_devices=1)
    args = [nc.dram_tensor(n, a.shape, F32, kind="ExternalInput").ap() for n, a in ins.items()]
    args += [nc.dram_tensor(n, s, F32, kind="ExternalOutput").ap() for n, s in outs.items()]
    fusion_kernel(nc, *args)
    got = run_bass_kernel_spmd(nc, [ins], core_ids=[0]).results[0]

    w = got["out_win"].reshape(2, WIN, PAIRS, D).transpose(2, 0, 1, 3).reshape(B, WIN, D)
    r = np.concatenate([got["out_rest"].reshape(P, RT, D).transpose(1, 0, 2).reshape(RT * P, D),
                        got["out_rest_last"]]).reshape(B, S - WIN, D)
    return np.concatenate([w[:, NPATCH:NPATCH + 1], w[:, :NPATCH], w[:, NPATCH + 1:], r], axis=1)
```

```python
from contextlib import ExitStack

import concourse.bass as bass
from concourse import mybir

F32 = mybir.dt.float32
F32R = mybir.dt.float32r
F16 = mybir.dt.float16
BF16 = mybir.dt.bfloat16
U32 = mybir.dt.uint32
ALU = mybir.AluOpType
ACT = mybir.ActivationFunctionType
AX_X = mybir.AxisListType.X

P = 128
D = 256
KD = D // P
B = 32
S = 114
WIN = 64
NPATCH = 36
FEAT = 768
KF = FEAT // P
HEADS = 16
DH = D // HEADS
NE = 8
GB = 4
PAIRS = B // 2
NG = B // GB
NREST = B * (S - WIN)
RT = NREST // P
RLAST = NREST - RT * P
CH = NE * D // 512
TXT_WIN = WIN - NPATCH - 1
EPS = 1e-5


def fusion_kernel(nc, xT, wlinT, posT, blin, cls, txt_win, rest, rest_last, wq, wk, wv, wo,
                  gateT, expT, consts, out_win, out_rest, out_rest_last):
    ctx = ExitStack()
    with ctx:
        def sb(name, shape, dt=F32):
            return ctx.enter_context(nc.sbuf_tensor(name, shape, dt))

        def bank(name, shape):
            return ctx.enter_context(nc.psum_tensor(name, shape, F32))

        def sem(name):
            return ctx.enter_context(nc.semaphore(name))

        const = sb("const", [P, P + 4 + NE])
        ident = const[:, 0:P]
        head_mask = const[:, P:P + 4]
        iota_e = const[:, P + 4:P + 4 + NE]
        eps_col = sb("eps_col", [P, 4])
        wlin = sb("wlin", [P, KF, D])
        pos = sb("pos", [P, KD, NPATCH + 1])
        bias = sb("bias", [P, KD])
        clst = sb("clst", [P, KD])
        patch_add = sb("patch_add", [P, KD, NPATCH])
        w_raw = sb("w_raw", [P, 4, KD, D])
        w_hi = sb("w_hi", [P, 4, KD, D], F32R)
        w_lo = sb("w_lo", [P, 4, KD, D], F32R)
        g_raw = sb("g_raw", [P, KD, NE])
        g_split = sb("g_split", [P, KD, NE, 2], F32R)
        e_raw = sb("e_raw", [P, KD, NE * D])
        e_hi = sb("e_hi", [P, KD, NE * D], F32R)
        e_lo = sb("e_lo", [P, KD, NE * D], F32R)

        win = sb("win", [P, PAIRS * D])
        rst = sb("rst", [P, (RT + 1) * D])

        xg = sb("xg", [P, KF, GB * NPATCH])
        hT = sb("hT", [P, KD, GB, WIN])
        norm_1 = sb("norm_1", [P, 2, D])
        x1_hi = sb("x1_hi", [P, KD, 2 * P], F32R)
        x1_lo = sb("x1_lo", [P, KD, 2 * P], F32R)
        q_bd = sb("q_bd", [P, KD, GB, 2, WIN])
        k_bd = sb("k_bd", [P, KD, GB, 4, WIN])
        v_bd = [sb(f"v_bd{n}", [P, 2 * 8, 2, 32], BF16) for n in range(3)]
        v_rest = sb("v_rest", [P, 2 * 8, 32])

        neg_max = sb("neg_max", [P, 2, 8])
        prob = sb("prob", [P, 8, 2, WIN])
        ssum = sb("ssum", [P, 8, 2])
        sinv = sb("sinv", [P, 8, 2])
        pT_hi = sb("pT_hi", [P, 8, P], F16)
        pT_lo = sb("pT_lo", [P, 8, P], F16)
        attn = sb("attn", [P, 2, 8, DH])
        cT_hi = sb("cT_hi", [P, 2, 2, WIN], F32R)
        cT_lo = sb("cT_lo", [P, 2, 2, WIN], F32R)

        norm_2 = sb("norm_2", [P, 3, D])
        x2_hi = sb("x2_hi", [P, 3, KD, P], F32R)
        x2_lo = sb("x2_lo", [P, 3, KD, P], F32R)
        logit = sb("logit", [P, 3, NE])
        top8 = sb("top8", [P, 3, 8])
        topi = sb("topi", [P, 3, 8], U32)
        topf = sb("topf", [P, 3, 2])
        wexp = sb("wexp", [P, 3, 4])
        wsel = sb("wsel", [P, 3, 2, NE])
        wfull = sb("wfull", [P, 3, NE])

        bn = sb("bn", [P, 5, 6])
        mv = sb("mv", [P, 5, 2])
        ve = sb("ve", [P, 5])
        rstd = sb("rstd", [P, 5])
        shift = sb("shift", [P, 5])

        SP_ = bank("score_bank", [P, 2, 512])
        O_ = bank("value_bank", [P, 8, 2, 2, DH])
        T_ = bank("norm_t_bank", [P, KD, P])
        U_ = bank("small_bank", [P, 512])
        PR = bank("proj_bank", [P, 512])
        XB = [bank(f"expert_bank{n}", [P, 512]) for n in range(2)]

        names = """d_const d_wlin d_embc d_x d_txt0 d_txt d_rest0 d_rest d_attw d_gate d_exp d_out
            zeroed consts_ready patch_const
            attw_hi attw_lo gate_hi gate_lo exp_hi exp_lo_a exp_lo_b
            emb_done emb_added hT_done win_added
            bn1 mv1 rstd1_ve rstd1_pow rstd1 norm1_ready x1T_done x1_hi_done x1_lo_done
            q_done q_taken k_done k_taken v_done v1_taken vr_ready v2_ready v3_ready
            score_done max_done exp_done inv_done
            pT_done pT_hi_done pT_lo_done pv_done attn_ready cT_done cT_hi_done cT_lo_done
            wo_done res_done bnw mvw rstdw_ve rstdw_pow rstdw
            bnr mvr rstdr_ve rstdr_pow rstdr
            norm2_ready x2T_done x2_hi_done x2_lo_done
            logit_done top_val logit_taken index_done ex_done gi_done gd_done g0_done g1_done gm_done gs_done
            weights_ready chunk_done chunk_part chunk_used"""
        m = {n: sem(n) for n in names.split()}

        def wait(eng, name, value):
            if not (isinstance(value, int) and value <= 0):
                eng.wait_ge(m[name], value)

        def wait_apart(eng, name, value):
            if not isinstance(value, int):
                eng.wait_ge(m["consts_ready"], 1)
            wait(eng, name, value)

        def win_at(t):
            return win[:, bass.ds(t * D, D)]

        def rst_at(r, rows=P):
            return rst[0:rows, bass.ds(r * D, D)]

        def tile_no(s, slot):
            return 0 if isinstance(s, int) and s == 0 else 3 * s - 2 + slot

        R_TAIL = NG + 1
        X_TAIL = 3 * NG + 1

        def tail(r):
            return X_TAIL + r - R_TAIL, (r - R_TAIL) % 3, P if r < RT else RLAST

        def is_at(s, n):
            return isinstance(s, int) and s == n

        def first(s):
            return is_at(s, 0)

        def attends(s):
            return not is_at(s, NG)

        def prepares(s):
            return not (is_at(s, NG) or is_at(s, NG - 1))

        def supersteps(eng, body):
            body(0)
            with eng.Fori(1, NG - 1) as s:
                body(s)
            body(NG - 1)
            body(NG)

        block = ctx.enter_context(nc.Block())

        @block.sync
        def _(sp):
            sp.dma_start(const[:], consts).then_inc(m["d_const"], 16)
            sp.dma_start(xg[:], xT[0]).then_inc(m["d_x"], 16)
            sp.dma_start(wlin[:], wlinT).then_inc(m["d_wlin"], 16)
            sp.wait_ge(m["zeroed"], 1)
            for cols, name in ((slice(0, 2 * D), "d_txt0"), (slice(2 * D, PAIRS * D), "d_txt")):
                for b in range(2):
                    sp.dma_start(win[WIN * b + NPATCH + 1:WIN * (b + 1), cols],
                                 txt_win[b, :, cols]).then_inc(m[name], 16)
                if name == "d_txt0":
                    sp.dma_start(e_raw[:], expT).then_inc(m["d_exp"], 16)
            sp.dma_start(rst[:, D:RT * D], rest[:, D:RT * D]).then_inc(m["d_rest"], 16)
            sp.dma_start(rst[0:RLAST, RT * D:(RT + 1) * D], rest_last).then_inc(m["d_rest"], 16)

            def load_patches(s):
                wait(sp, "emb_done", s + 2)
                sp.dma_start(xg[:], xT[s + 2] if isinstance(s, int) else
                             xT[bass.ds(s + 2, 1)].squeeze(0)).then_inc(m["d_x"], 16)

            def store_rest(x, r):
                wait(sp, "chunk_used", CH * (x + 1))
                sp.dma_start(out_rest[:, bass.ds(r * D, D)], rst_at(r)).then_inc(m["d_out"], 16)

            def store_win(x, t):
                wait(sp, "chunk_used", CH * (x + 1))
                sp.dma_start(out_win[:, bass.ds(t * D, D)], win_at(t)).then_inc(m["d_out"], 16)

            wait(sp, "emb_done", 1)
            sp.dma_start(xg[:], xT[1]).then_inc(m["d_x"], 16)

            def superstep(s):
                if not (is_at(s, NG - 2) or is_at(s, NG - 1) or is_at(s, NG)):
                    load_patches(s)
                store_rest(tile_no(s, 0), s)
                if not first(s):
                    store_win(tile_no(s, 1), 2 * s - 2)
                    store_win(tile_no(s, 2), 2 * s - 1)

            superstep(0)
            with sp.Fori(1, NG - 2) as s:
                superstep(s)
            for s in (NG - 2, NG - 1, NG):
                superstep(s)
            for r in range(R_TAIL, RT):
                store_rest(tail(r)[0], r)
            wait(sp, "chunk_used", CH * (tail(RT)[0] + 1))
            sp.dma_start(out_rest_last, rst_at(RT, RLAST)).then_inc(m["d_out"], 16)
            sp.wait_ge(m["d_out"], 16 * (PAIRS + RT + 1))

        @block.gpsimd
        def _(pool):
            pool.memset(win[:], 0.0).then_inc(m["zeroed"], 1)
            pool.memset(hT[:], 0.0).then_inc(m["zeroed"], 1)
            pool.memset(eps_col[:, 0:1], EPS)
            pool.memset(eps_col[:, 1:2], -0.5)
            pool.memset(eps_col[:, 3:4], -1.0)
            pool.memset(eps_col[:, 2:3], 1.0).then_inc(m["consts_ready"], 1)
            pool.wait_ge(m["consts_ready"], 1)

            def inverse_deviation(kind, n, slot, rows=P):
                wait(pool, {"rstd1": "mv1", "rstdw": "mvw", "rstdr": "mvr"}[kind], n + 1)
                pool.tensor_tensor(ve[0:rows, slot:slot + 1], mv[0:rows, slot, 1:2], eps_col[0:rows, 0:1],
                                   ALU.add).then_inc(m[kind + "_ve"], 1)
                wait(pool, kind + "_ve", n + 1)
                pool.tensor_tensor(rstd[0:rows, slot:slot + 1], ve[0:rows, slot:slot + 1],
                                   eps_col[0:rows, 1:2], ALU.pow).then_inc(m[kind + "_pow"], 1)
                wait_apart(pool, kind + "_pow", n + 1)
                pool.tensor_scalar(shift[0:rows, slot:slot + 1], mv[0:rows, slot, 0:1], -1.0,
                                   rstd[0:rows, slot:slot + 1], ALU.mult, ALU.mult).then_inc(m[kind], 1)

            def gate(x, slot, rows=P):
                e, den, w0, w1 = (wexp[0:rows, slot, n:n + 1] for n in range(4))
                wait(pool, "ex_done", x + 1)
                pool.tensor_tensor(den, e, eps_col[0:rows, 2:3], ALU.add).then_inc(m["gd_done"], 1)
                wait_apart(pool, "index_done", x + 1)
                pool.tensor_copy(topf[0:rows, slot], topi[0:rows, slot, 0:2]).then_inc(m["gi_done"], 1)
                wait(pool, "gd_done", x + 1)
                pool.tensor_tensor(w0, den, eps_col[0:rows, 3:4], ALU.pow).then_inc(m["g0_done"], 1)
                wait(pool, "g0_done", x + 1)
                pool.tensor_tensor(w1, e, w0, ALU.mult).then_inc(m["g1_done"], 1)
                wait_apart(pool, "g1_done", x + 1)
                wait(pool, "gi_done", x + 1)
                for n, w in enumerate((w0, w1)):
                    pool.tensor_scalar(wsel[0:rows, slot, n], iota_e[0:rows], topf[0:rows, slot, n:n + 1], w,
                                       ALU.is_equal, ALU.mult).then_inc(m["gm_done"], 1)
                wait(pool, "gm_done", 2 * (x + 1))
                pool.tensor_tensor(wfull[0:rows, slot], wsel[0:rows, slot, 0], wsel[0:rows, slot, 1],
                                   ALU.add).then_inc(m["weights_ready"], 1)

            def last_v_part(g, before, count):
                wait(pool, before, count)
                wait(pool, "v2_ready", 2 * (g + 1))
                wait(pool, "vr_ready", 2 * (g + 1))
                for b in range(2):
                    h = slice(WIN * b, WIN * (b + 1))
                    pool.tensor_tensor(v_bd[2][h, :, b], v_rest[h], v_bd[1][h, :, b],
                                       ALU.subtract).then_inc(m["v3_ready"], 1)
                    wait(pool, "v3_ready", 2 * g + b + 1)

            pool.wait_ge(m["d_const"], 16)
            inverse_deviation("rstdr", 0, 4)
            inverse_deviation("rstd1", 0, 0)
            inverse_deviation("rstd1", 1, 1)
            gate(0, 0)
            pool.wait_ge(m["exp_hi"], 2)
            for n in range(4):
                c = slice(n * 512, (n + 1) * 512)
                pool.tensor_tensor(e_lo[:, 1, c], e_raw[:, 1, c], e_hi[:, 1, c].bitcast(F32),
                                   ALU.subtract).then_inc(m["exp_lo_b"], 1)
            pool.wait_ge(m["patch_const"], 1)
            last_v_part(0, "exp_lo_b", 4)

            def superstep(s):
                if not first(s):
                    gate(tile_no(s, 1), 1)
                if prepares(s):
                    inverse_deviation("rstd1", 2 * (s + 1), 0)
                    inverse_deviation("rstd1", 2 * (s + 1) + 1, 1)
                inverse_deviation("rstdr", s + 1, 4)
                if attends(s):
                    inverse_deviation("rstdw", 2 * s, 2)
                if not first(s):
                    gate(tile_no(s, 2), 2)
                gate(tile_no(s + 1, 0), 0)
                if attends(s):
                    inverse_deviation("rstdw", 2 * s + 1, 3)
                if prepares(s):
                    last_v_part(s + 1, "rstdw", 2 * s + 2)

            supersteps(pool, superstep)
            for r in range(R_TAIL, RT):
                inverse_deviation("rstdr", r + 1, 4, tail(r + 1)[2])
                gate(*tail(r + 1))

        @block.scalar
        def _(act):
            act.dma_start(rst[:, 0:D], rest[:, 0:D]).then_inc(m["d_rest0"], 16)
            act.dma_start(pos[:], posT).then_inc(m["d_embc"], 16)
            act.dma_start(bias[:], blin).then_inc(m["d_embc"], 16)
            act.dma_start(clst[:], cls).then_inc(m["d_embc"], 16)
            for n, w in enumerate((wq, wk, wv, wo)):
                act.dma_start(w_raw[:, n], w).then_inc(m["d_attw"], 16)
            act.dma_start(g_raw[:], gateT).then_inc(m["d_gate"], 16)

            def copy(out, in_, **kw):
                return act.activation(out, in_, ACT.Copy, **kw)

            def normalise(out, src, n, rows=P):
                return act.activation(out, src, ACT.Identity, scale=rstd[0:rows, n:n + 1],
                                      bias=shift[0:rows, n:n + 1])

            def norm1(g, j):
                wait(act, "rstd1", 2 * g + j + 1)
                normalise(norm_1[:, j], win_at(2 * g + j), j).then_inc(m["norm1_ready"], 1)

            def norm2_win(slot, t):
                wait(act, "rstdw", t + 1)
                normalise(norm_2[:, slot], win_at(t), 1 + slot).then_inc(m["norm2_ready"], 1)

            def norm2_rest(slot, r, rows=P):
                wait(act, "rstdr", r + 1)
                normalise(norm_2[0:rows, slot], rst_at(r, rows), 4, rows).then_inc(m["norm2_ready"], 1)

            def norm2_hi(x, slot, rows=P):
                wait(act, "x2T_done", x + 1)
                copy(x2_hi[:, slot, :, 0:rows], T_[:, :, 0:rows]).then_inc(m["x2_hi_done"], 1)

            def gate_exp(x, slot, rows=P):
                wait(act, "top_val", x + 1)
                act.activation(wexp[0:rows, slot, 0:1], top8[0:rows, slot, 0:1], ACT.Exp, scale=-1.0,
                               bias=top8[0:rows, slot, 1:2]).then_inc(m["ex_done"], 1)

            def softmax_exp(t, b):
                if b == 0:
                    wait(act, "max_done", t + 1)
                for c in range(8):
                    i = act.activation(prob[:, c, b], SP_[:, b, WIN * c:WIN * (c + 1)], ACT.Exp,
                                       bias=neg_max[:, b, c:c + 1], accum_out=ssum[:, c, b:b + 1])
                if b == 1:
                    i.then_inc(m["exp_done"], 1)

            def prob_hi(t):
                wait(act, "pT_done", t + 1)
                copy(pT_hi[:].rearrange("p c q -> p (c q)"),
                     SP_[:].rearrange("p b n -> p (b n)")).then_inc(m["pT_hi_done"], 1)

            def context_hi(t):
                wait(act, "cT_done", t + 1)
                copy(cT_hi[:].rearrange("p h b q -> p b h q"),
                     U_[:, 0:D].rearrange("p (b h q) -> p b h q", b=2, h=2)).then_inc(m["cT_hi_done"], 1)

            def norm1_hi(g, j):
                wait(act, "x1T_done", 2 * g + j + 1)
                copy(x1_hi[:, :, P * j:P * (j + 1)], T_[:]).then_inc(m["x1_hi_done"], 1)

            def take_q(g):
                wait(act, "q_done", g + 1)
                if first(g):
                    act.wait_ge(m["patch_const"], 1)
                src = PR[:].rearrange("p (n q) -> p n q", q=WIN)
                for hs in range(2):
                    h = slice(WIN * hs, WIN * (hs + 1))
                    copy(q_bd[h].rearrange("p c b h q -> p (c b) h q")[:, :, hs], src[h],
                         scale=DH ** -0.5).then_inc(m["q_taken"], 1)

            def take_k(g):
                wait(act, "k_done", g + 1)
                src = PR[:].rearrange("p (n q) -> p n q", q=WIN)
                for hh in range(4):
                    copy(k_bd[:].rearrange("p c b h k -> p (c b) h k")[:, :, hh], src,
                         scale=head_mask[:, hh:hh + 1]).then_inc(m["k_taken"], 1)

            def take_v(g):
                wait(act, "v_done", g + 1)
                src = PR[:].rearrange("p (n d) -> p n d", d=32)
                for b in range(2):
                    h = slice(WIN * b, WIN * (b + 1))
                    copy(v_bd[0][h, :, b], src[h]).then_inc(m["v1_taken"], 1)

            def second_v_part(g):
                wait(act, "vr_ready", 2 * (g + 1))
                for b in range(2):
                    h = slice(WIN * b, WIN * (b + 1))
                    copy(v_bd[1][h, :, b], v_rest[h]).then_inc(m["v2_ready"], 1)

            norm2_rest(0, 0)
            norm2_hi(0, 0)
            act.wait_ge(m["d_attw"], 64)
            act.wait_ge(m["d_const"], 16)
            copy(w_hi[:].rearrange("p a b c -> p (a b c)"),
                 w_raw[:].rearrange("p a b c -> p (a b c)")).then_inc(m["attw_hi"], 1)
            act.wait_ge(m["d_gate"], 16)
            copy(g_split[:, :, :, 0], g_raw[:]).then_inc(m["gate_hi"], 1)
            norm1(0, 0)
            norm1(0, 1)
            norm1_hi(0, 0)
            norm1_hi(0, 1)
            take_q(0)
            gate_exp(0, 0)
            take_k(0)
            act.wait_ge(m["d_exp"], 16)
            copy(e_hi[:, 0], e_raw[:, 0]).then_inc(m["exp_hi"], 1)
            take_v(0)
            copy(e_hi[:, 1], e_raw[:, 1]).then_inc(m["exp_hi"], 1)
            second_v_part(0)

            def superstep(s):
                if not first(s):
                    norm2_hi(tile_no(s, 1), 1)
                if attends(s):
                    softmax_exp(2 * s, 0)
                    softmax_exp(2 * s, 1)
                if not first(s):
                    gate_exp(tile_no(s, 1), 1)
                if prepares(s):
                    norm1(s + 1, 0)
                    norm1(s + 1, 1)
                if attends(s):
                    prob_hi(2 * s)
                if not first(s):
                    norm2_win(2, 2 * s - 1)
                if prepares(s):
                    norm1_hi(s + 1, 0)
                    norm1_hi(s + 1, 1)
                if attends(s):
                    softmax_exp(2 * s + 1, 0)
                    context_hi(2 * s)
                if not first(s):
                    norm2_hi(tile_no(s, 2), 2)
                if attends(s):
                    softmax_exp(2 * s + 1, 1)
                if prepares(s):
                    take_q(s + 1)
                if not first(s):
                    gate_exp(tile_no(s, 2), 2)
                if attends(s):
                    prob_hi(2 * s + 1)
                norm2_rest(0, s + 1)
                if prepares(s):
                    take_k(s + 1)
                norm2_hi(tile_no(s + 1, 0), 0)
                if attends(s):
                    norm2_win(1, 2 * s)
                if prepares(s):
                    take_v(s + 1)
                gate_exp(tile_no(s + 1, 0), 0)
                if attends(s):
                    context_hi(2 * s + 1)
                if prepares(s):
                    second_v_part(s + 1)

            supersteps(act, superstep)
            for r in range(R_TAIL, RT):
                x, slot, rows = tail(r + 1)
                norm2_rest(slot, r + 1, rows)
                norm2_hi(x, slot, rows)
                gate_exp(x, slot, rows)

        @block.vector
        def _(dve):
            def stats(kind, n, slot, src, rows=P):
                bn_sem, mv_sem = {"1": ("bn1", "mv1"), "w": ("bnw", "mvw"), "r": ("bnr", "mvr")}[kind]
                dve.bn_stats(bn[0:rows, slot], src).then_inc(m[bn_sem], 1)
                wait_apart(dve, bn_sem, n + 1)
                dve.bn_aggr(mv[0:rows, slot], bn[0:rows, slot]).then_inc(m[mv_sem], 1)

            def norm2_lo(x, slot, rows=P):
                wait(dve, "x2_hi_done", x + 1)
                dve.tensor_tensor(x2_lo[:, slot, :, 0:rows], T_[:, :, 0:rows],
                                  x2_hi[:, slot, :, 0:rows].bitcast(F32), ALU.subtract).then_inc(m["x2_lo_done"], 1)

            def top_two(x, slot, rows=P):
                wait(dve, "logit_done", x + 1)
                lg = logit[0:rows, slot]
                dve.reduce_sum(lg, U_[0:rows, 0:2 * NE].rearrange("p (e n) -> p e n", n=2),
                               AX_X).then_inc(m["logit_taken"], 1)
                wait_apart(dve, "logit_taken", x + 1)
                dve.max(top8[0:rows, slot], lg).then_inc(m["top_val"], 1)
                wait_apart(dve, "top_val", x + 1)
                dve.max_index(topi[0:rows, slot], top8[0:rows, slot], lg).then_inc(m["index_done"], 1)

            def experts(x, slot, c, acc, rows=P):
                if c == 0:
                    wait(dve, "weights_ready", x + 1)
                wait(dve, "chunk_done", CH * x + c + 1)
                for n in range(2):
                    e = 2 * c + n
                    i = dve.scalar_tensor_tensor(out=acc, in0=XB[c % 2][0:rows, D * n:D * (n + 1)],
                                                 scalar=wfull[0:rows, slot, e:e + 1], in1=acc,
                                                 op0=ALU.mult, op1=ALU.add)
                    if n == 0:
                        i.then_inc(m["chunk_part"], 1)
                        wait(dve, "chunk_part", CH * x + c + 1)
                i.then_inc(m["chunk_used"], 1)
                if c < CH - 1:
                    wait(dve, "chunk_used", CH * x + c + 1)

            def take_embedding(g):
                wait(dve, "emb_done", g + 1)
                src = PR[:, 0:KD * GB * NPATCH].rearrange("p (c b n) -> p c b n", c=KD, b=GB)
                dve.tensor_tensor(hT[:, :, :, 0:NPATCH], src,
                                  patch_add[:].unsqueeze(2).to_broadcast([P, KD, GB, NPATCH]),
                                  ALU.add).then_inc(m["emb_added"], 1)

            def add_window(g, j):
                t = 2 * g + j
                wait(dve, "hT_done", t + 1)
                dve.tensor_tensor(win_at(t), U_[:, 0:D], win_at(t), ALU.add).then_inc(m["win_added"], 1)
                wait_apart(dve, "win_added", t + 1)
                stats("1", t, j, win_at(t))

            def norm1_lo(g, j):
                wait(dve, "x1_hi_done", 2 * g + j + 1)
                c = slice(P * j, P * (j + 1))
                dve.tensor_tensor(x1_lo[:, :, c], T_[:], x1_hi[:, :, c].bitcast(F32),
                                  ALU.subtract).then_inc(m["x1_lo_done"], 1)

            def softmax_max(t):
                wait(dve, "score_done", t + 1)
                s = SP_[:].rearrange("p b (c k) -> p (b c) k", k=WIN)
                dve.tensor_reduce(neg_max[:].rearrange("p b c -> p (b c)"), s, AX_X, ALU.max,
                                  negate=True).then_inc(m["max_done"], 1)

            def softmax_inverse(t):
                wait(dve, "exp_done", t + 1)
                dve.reciprocal(sinv[:], ssum[:]).then_inc(m["inv_done"], 1)

            def prob_lo(t):
                wait(dve, "pT_hi_done", t + 1)
                dve.tensor_tensor(pT_lo[:].rearrange("p c q -> p (c q)"), SP_[:].rearrange("p b n -> p (b n)"),
                                  pT_hi[:].rearrange("p c q -> p (c q)"), ALU.subtract).then_inc(m["pT_lo_done"], 1)

            def take_context(t):
                wait(dve, "pv_done", t + 1)
                wait(dve, "inv_done", t + 1)
                for hs in range(2):
                    h = slice(WIN * hs, WIN * (hs + 1))
                    dve.tensor_tensor(attn[h].rearrange("p b c d -> p c b d"), O_[h, :, :, hs],
                                      sinv[h].unsqueeze(3)
                                      .to_broadcast([WIN, 8, 2, DH]), ALU.mult).then_inc(m["attn_ready"], 1)

            def context_lo(t):
                wait(dve, "cT_hi_done", t + 1)
                dve.tensor_tensor(cT_lo[:].rearrange("p h b q -> p b h q"),
                                  U_[:, 0:D].rearrange("p (b h q) -> p b h q", b=2, h=2),
                                  cT_hi[:].rearrange("p h b q -> p b h q").bitcast(F32),
                                  ALU.subtract).then_inc(m["cT_lo_done"], 1)

            def add_attention(s, j):
                t = 2 * s + j
                wait(dve, "wo_done", t + 1)
                dve.tensor_tensor(win_at(t), U_[:, 0:D], win_at(t), ALU.add).then_inc(m["res_done"], 1)
                wait_apart(dve, "res_done", t + 1)
                stats("w", t, 2 + j, win_at(t))

            def v_minus_first(g):
                wait(dve, "v1_taken", 2 * (g + 1))
                src = PR[:].rearrange("p (n d) -> p n d", d=32)
                for b in range(2):
                    h = slice(WIN * b, WIN * (b + 1))
                    dve.tensor_tensor(v_rest[h], src[h], v_bd[0][h, :, b], ALU.subtract).then_inc(m["vr_ready"], 1)

            dve.memset(q_bd[:], 0.0)
            for n in range(3):
                dve.memset(v_bd[n][:], 0.0)
            dve.wait_ge(m["d_embc"], 48)
            for c in range(KD):
                dve.tensor_scalar(patch_add[:, c], pos[:, c, 1:NPATCH + 1], bias[:, c:c + 1], None, ALU.add)
            dve.wait_ge(m["zeroed"], 2)
            dve.tensor_tensor(hT[:, :, :, NPATCH:NPATCH + 1],
                              pos[:, :, 0:1].unsqueeze(2).to_broadcast([P, KD, GB, 1]),
                              clst[:].unsqueeze(2).unsqueeze(3).to_broadcast([P, KD, GB, 1]),
                              ALU.add).then_inc(m["patch_const"], 1)
            dve.wait_ge(m["d_rest0"], 16)
            stats("r", 0, 4, rst_at(0))
            dve.wait_ge(m["patch_const"], 1)
            norm2_lo(0, 0)
            take_embedding(0)
            dve.wait_ge(m["d_txt0"], 32)
            for j in range(2):
                add_window(0, j)
            dve.wait_ge(m["attw_hi"], 1)
            dve.tensor_tensor(w_lo[:].rearrange("p a b c -> p (a b c)"), w_raw[:].rearrange("p a b c -> p (a b c)"),
                              w_hi[:].rearrange("p a b c -> p (a b c)").bitcast(F32),
                              ALU.subtract).then_inc(m["attw_lo"], 1)
            dve.wait_ge(m["gate_hi"], 1)
            dve.tensor_tensor(g_split[:, :, :, 1], g_raw[:], g_split[:, :, :, 0].bitcast(F32),
                              ALU.subtract).then_inc(m["gate_lo"], 1)
            for j in range(2):
                norm1_lo(0, j)
            top_two(0, 0)
            dve.wait_ge(m["exp_hi"], 1)
            dve.tensor_tensor(e_lo[:, 0], e_raw[:, 0], e_hi[:, 0].bitcast(F32),
                              ALU.subtract).then_inc(m["exp_lo_a"], 1)
            v_minus_first(0)
            dve.wait_ge(m["d_txt"], 32)
            dve.wait_ge(m["d_rest"], 32)

            def superstep(s):
                x = [tile_no(s, n) for n in range(3)]
                acc = [rst_at(s), None, None] if first(s) else [rst_at(s), win_at(2 * s - 2), win_at(2 * s - 1)]
                if attends(s):
                    softmax_max(2 * s)
                if not first(s):
                    norm2_lo(x[1], 1)
                if prepares(s):
                    take_embedding(s + 1)
                experts(x[0], 0, 0, acc[0])
                if not first(s):
                    top_two(x[1], 1)
                experts(x[0], 0, 1, acc[0])
                if prepares(s):
                    add_window(s + 1, 0)
                experts(x[0], 0, 2, acc[0])
                if prepares(s):
                    add_window(s + 1, 1)
                stats("r", s + 1, 4, rst_at(s + 1))
                if attends(s):
                    prob_lo(2 * s)
                    softmax_inverse(2 * s)
                experts(x[0], 0, 3, acc[0])
                if not first(s):
                    experts(x[1], 1, 0, acc[1])
                if attends(s):
                    take_context(2 * s)
                if prepares(s):
                    norm1_lo(s + 1, 0)
                if attends(s):
                    softmax_max(2 * s + 1)
                if prepares(s):
                    norm1_lo(s + 1, 1)
                if not first(s):
                    experts(x[1], 1, 1, acc[1])
                if attends(s):
                    context_lo(2 * s)
                if not first(s):
                    norm2_lo(x[2], 2)
                    experts(x[1], 1, 2, acc[1])
                if attends(s):
                    add_attention(s, 0)
                if not first(s):
                    experts(x[1], 1, 3, acc[1])
                    top_two(x[2], 2)
                if attends(s):
                    prob_lo(2 * s + 1)
                    softmax_inverse(2 * s + 1)
                if not first(s):
                    experts(x[2], 2, 0, acc[2])
                if attends(s):
                    take_context(2 * s + 1)
                norm2_lo(tile_no(s + 1, 0), 0)
                top_two(tile_no(s + 1, 0), 0)
                if prepares(s):
                    v_minus_first(s + 1)
                if not first(s):
                    experts(x[2], 2, 1, acc[2])
                if attends(s):
                    context_lo(2 * s + 1)
                if not first(s):
                    experts(x[2], 2, 2, acc[2])
                if attends(s):
                    add_attention(s, 1)
                if not first(s):
                    experts(x[2], 2, 3, acc[2])

            supersteps(dve, superstep)
            for r in range(R_TAIL, RT + 1):
                x, slot, rows = tail(r)
                acc = rst_at(r, rows)
                more = r < RT
                if more:
                    nx, nslot, nrows = tail(r + 1)
                    stats("r", r + 1, 4, rst_at(r + 1, nrows), nrows)
                experts(x, slot, 0, acc, rows)
                if more:
                    norm2_lo(nx, nslot, nrows)
                experts(x, slot, 1, acc, rows)
                if more:
                    top_two(nx, nslot, nrows)
                experts(x, slot, 2, acc, rows)
                experts(x, slot, 3, acc, rows)

        @block.tensor
        def _(pe):
            def split_product(out, terms, count=None):
                n = 0
                for (lh, ll), (rh, rl) in terms:
                    for lhs, rhs in ((lh, rh), (lh, rl), (ll, rh)):
                        n += 1
                        i = pe.matmul(out, lhs, rhs, start=(n == 1), stop=(n == 3 * len(terms)))
                return i

            def transpose_norm2(x, slot, rows=P):
                wait(pe, "norm2_ready", x + 1)
                for k in range(KD):
                    i = pe.transpose(T_[:, k, 0:rows], norm_2[0:rows, slot, P * k:P * (k + 1)],
                                     ident[0:rows, 0:rows])
                i.then_inc(m["x2T_done"], 1)

            def x2(slot, k, rows):
                return x2_hi[:, slot, k, 0:rows], x2_lo[:, slot, k, 0:rows]

            def logits(x, slot, rows=P):
                wait(pe, "x2_lo_done", x + 1)
                terms = [(part, k) for k in range(KD) for part in x2(slot, k, rows)]
                for n, (part, k) in enumerate(terms):
                    i = pe.matmul(U_[0:rows, 0:2 * NE], part, g_split[:, k].rearrange("p e n -> p (e n)"),
                                  start=(n == 0), stop=(n == len(terms) - 1))
                i.then_inc(m["logit_done"], 1)

            def experts(x, slot, c, rows=P):
                wait(pe, "chunk_used", CH * x + c - 1)
                w = slice(512 * c, 512 * (c + 1))
                split_product(XB[c % 2][0:rows], [(x2(slot, k, rows), (e_hi[:, k, w], e_lo[:, k, w]))
                                                  for k in range(KD)]).then_inc(m["chunk_done"], 1)

            def embed(g):
                wait(pe, "d_x", 16 * (g + 1))
                for c in range(KD):
                    for k in range(KF):
                        i = pe.matmul(PR[:, GB * NPATCH * c:GB * NPATCH * (c + 1)], wlin[:, k, P * c:P * (c + 1)],
                                      xg[:, k], start=(k == 0), stop=(k == KF - 1))
                i.then_inc(m["emb_done"], 1)

            def embed_back(g, j):
                wait(pe, "emb_added", g + 1)
                for c in range(KD):
                    i = pe.transpose(U_[:, P * c:P * (c + 1)],
                                     hT[:, c, 2 * j:2 * j + 2].rearrange("p b n -> p (b n)"), ident)
                i.then_inc(m["hT_done"], 1)

            def transpose_norm1(g, j):
                wait(pe, "norm1_ready", 2 * g + j + 1)
                for k in range(KD):
                    i = pe.transpose(T_[:, k], norm_1[:, j, P * k:P * (k + 1)], ident)
                i.then_inc(m["x1T_done"], 1)

            def w_pair(n, k, cols):
                return w_hi[:, n, k, cols], w_lo[:, n, k, cols]

            def project(g, n, name):
                for c in range(KD):
                    i = split_product(PR[:, 2 * P * c:2 * P * (c + 1)],
                                      [(w_pair(n, k, slice(P * c, P * (c + 1))), (x1_hi[:, k], x1_lo[:, k]))
                                       for k in range(KD)])
                i.then_inc(m[name], 1)

            def project_v(g):
                for j in range(2):
                    c = slice(P * j, P * (j + 1))
                    i = split_product(PR[:, D * j:D * (j + 1)],
                                      [((x1_hi[:, k, c], x1_lo[:, k, c]), w_pair(2, k, slice(0, D)))
                                       for k in range(KD)])
                i.then_inc(m["v_done"], 1)

            def scores(s, j):
                t = 2 * s + j
                wait(pe, "q_taken", 2 * (s + 1))
                wait(pe, "k_taken", 4 * (s + 1))
                wait(pe, "pT_lo_done", t)
                for b in range(2):
                    for c in range(KD):
                        i = pe.matmul(SP_[:, b, D * c:D * (c + 1)],
                                      q_bd[:, c, 2 * j + b].rearrange("p h q -> p (h q)"),
                                      k_bd[:, c, 2 * j + b].rearrange("p h k -> p (h k)"), start=True, stop=True)
                i.then_inc(m["score_done"], 1)

            def transpose_prob(t):
                wait(pe, "exp_done", t + 1)
                pt = SP_[:].rearrange("p b (c q) -> p (b c) q", q=P)
                for c in range(8):
                    i = pe.transpose(pt[:, c], prob[:, c].rearrange("p b k -> p (b k)"), ident)
                i.then_inc(m["pT_done"], 1)

            def values(s, j):
                t = 2 * s + j
                wait(pe, "pT_lo_done", t + 1)
                wait(pe, "v3_ready", 2 * (s + 1))
                wait(pe, "attn_ready", 2 * t)
                for c in range(8):
                    terms = [(pT_hi, 0), (pT_hi, 1), (pT_hi, 2), (pT_lo, 0), (pT_lo, 1)]
                    for n, (pr, v) in enumerate(terms):
                        i = pe.matmul(O_[:, c].rearrange("p b h d -> p (b h d)"), pr[:, c],
                                      v_bd[v][:, 8 * j + c].rearrange("p b d -> p (b d)"),
                                      start=(n == 0), stop=(n == len(terms) - 1))
                i.then_inc(m["pv_done"], 1)

            def transpose_context(t):
                wait(pe, "attn_ready", 2 * (t + 1))
                for b in range(2):
                    i = pe.transpose(U_[:, P * b:P * (b + 1)], attn[:, b].rearrange("p c d -> p (c d)"), ident)
                i.then_inc(m["cT_done"], 1)

            def project_out(t):
                wait(pe, "cT_lo_done", t + 1)
                split_product(U_[:, 0:D],
                              [((cT_hi[:, h].rearrange("p b q -> p (b q)"), cT_lo[:, h].rearrange("p b q -> p (b q)")),
                                w_pair(3, h, slice(0, D))) for h in range(2)]).then_inc(m["wo_done"], 1)

            pe.wait_ge(m["d_const"], 16)
            transpose_norm2(0, 0)
            pe.wait_ge(m["d_wlin"], 16)
            embed(0)
            for j in range(2):
                wait(pe, "win_added", j)
                embed_back(0, j)
            wait(pe, "x2_lo_done", 1)
            transpose_norm1(0, 0)
            wait(pe, "x1_lo_done", 1)
            transpose_norm1(0, 1)
            wait(pe, "x1_lo_done", 2)
            pe.wait_ge(m["attw_lo"], 1)
            project(0, 0, "q_done")
            pe.wait_ge(m["gate_lo"], 1)
            wait(pe, "win_added", 2)
            logits(0, 0)
            wait(pe, "q_taken", 2)
            project(0, 1, "k_done")
            wait(pe, "k_taken", 4)
            project_v(0)

            def superstep(s):
                x = [tile_no(s, n) for n in range(3)]
                nx = tile_no(s + 1, 0)
                g = s + 1
                if attends(s):
                    scores(s, 0)
                if not first(s):
                    wait(pe, "x2_lo_done", x[1])
                    transpose_norm2(x[1], 1)
                if prepares(s):
                    wait(pe, "vr_ready", 2 * g)
                    embed(g)
                if first(s):
                    pe.wait_ge(m["exp_lo_a"], 1)
                    pe.wait_ge(m["exp_lo_b"], 4)
                experts(x[0], 0, 0)
                if not first(s):
                    wait(pe, "res_done", 2 * s)
                    logits(x[1], 1)
                experts(x[0], 0, 1)
                if prepares(s):
                    wait(pe, "logit_taken", 1 if first(s) else x[1] + 1)
                    embed_back(g, 0)
                experts(x[0], 0, 2)
                if prepares(s):
                    wait(pe, "win_added", 2 * g + 1)
                    embed_back(g, 1)
                if attends(s):
                    transpose_prob(2 * s)
                experts(x[0], 0, 3)
                if not first(s):
                    experts(x[1], 1, 0)
                if attends(s):
                    values(s, 0)
                if prepares(s):
                    wait(pe, "x2_lo_done", 1 if first(s) else x[1] + 1)
                    transpose_norm1(g, 0)
                if attends(s):
                    scores(s, 1)
                if prepares(s):
                    wait(pe, "x1_lo_done", 2 * g + 1)
                    transpose_norm1(g, 1)
                if not first(s):
                    experts(x[1], 1, 1)
                if attends(s):
                    if prepares(s):
                        wait(pe, "win_added", 2 * g + 2)
                    else:
                        wait(pe, "logit_taken", x[1] + 1)
                    transpose_context(2 * s)
                if prepares(s):
                    wait(pe, "x1_lo_done", 2 * g + 2)
                    project(g, 0, "q_done")
                else:
                    wait(pe, "x2_lo_done", x[2])
                if not first(s):
                    transpose_norm2(x[2], 2)
                    experts(x[1], 1, 2)
                if attends(s):
                    project_out(2 * s)
                if not first(s):
                    experts(x[1], 1, 3)
                    if attends(s):
                        wait(pe, "res_done", 2 * s + 1)
                    else:
                        wait(pe, "logit_taken", x[1] + 1)
                    logits(x[2], 2)
                if attends(s):
                    transpose_prob(2 * s + 1)
                if prepares(s):
                    wait(pe, "q_taken", 2 * (g + 1))
                    project(g, 1, "k_done")
                if not first(s):
                    experts(x[2], 2, 0)
                if attends(s):
                    values(s, 1)
                if not first(s):
                    wait(pe, "x2_lo_done", nx)
                transpose_norm2(nx, 0)
                if prepares(s):
                    wait(pe, "k_taken", 4 * (g + 1))
                    project_v(g)
                if first(s):
                    wait(pe, "res_done", 1)
                else:
                    wait(pe, "logit_taken", nx)
                logits(nx, 0)
                if not first(s):
                    experts(x[2], 2, 1)
                if attends(s):
                    wait(pe, "logit_taken", nx + 1)
                    transpose_context(2 * s + 1)
                if not first(s):
                    experts(x[2], 2, 2)
                if attends(s):
                    project_out(2 * s + 1)
                if not first(s):
                    experts(x[2], 2, 3)

            supersteps(pe, superstep)
            for r in range(R_TAIL, RT + 1):
                x, slot, rows = tail(r)
                more = r < RT
                experts(x, slot, 0, rows)
                if more:
                    wait(pe, "x2_lo_done", x + 1)
                    transpose_norm2(*tail(r + 1))
                experts(x, slot, 1, rows)
                if more:
                    wait(pe, "logit_taken", x + 1)
                    logits(*tail(r + 1))
                experts(x, slot, 2, rows)
                experts(x, slot, 3, rows)


def kernel(x, txt, L0_tok_W_lin, L0_tok_b_lin, L0_tok_class_token, L0_tok_position_embeddings,
           L0_attn_Wq, L0_attn_Wk, L0_attn_Wv, L0_attn_Wo, L0_ffn_gate_w, L0_ffn_expert_w):
    import numpy as np
    import concourse.bacc as bacc
    from concourse.bass_utils import run_bass_kernel_spmd

    def chunks(a):
        a = np.asarray(a)
        return np.ascontiguousarray(a.reshape(-1, P, a.shape[-1]).transpose(1, 0, 2))

    x, txt = np.asarray(x), np.asarray(txt)
    xT = x.reshape(NG, GB, 3, 6, 16, 6, 16).transpose(0, 2, 4, 6, 1, 3, 5).reshape(NG, KF, P, GB * NPATCH)
    pos = np.asarray(L0_tok_position_embeddings)[0]
    text_in = txt[:, :TXT_WIN].reshape(PAIRS, 2, TXT_WIN, D).transpose(1, 2, 0, 3).reshape(2, TXT_WIN, PAIRS * D)
    rest = txt[:, TXT_WIN:].reshape(NREST, D)
    wv = np.asarray(L0_attn_Wv).reshape(D, 2, 2, 4, DH).transpose(0, 1, 3, 2, 4).reshape(D, D)
    wo = np.asarray(L0_attn_Wo).reshape(2, 2, 4, DH, D).transpose(1, 0, 2, 3, 4).reshape(D, D)
    heads = (np.arange(P)[:, None] % WIN // DH == np.arange(4)[None]).astype(np.float32)
    consts = np.concatenate([np.eye(P, dtype=np.float32), heads,
                             np.tile(np.arange(NE, dtype=np.float32), (P, 1))], axis=1)
    ins = {
        "xT": np.ascontiguousarray(xT.transpose(0, 2, 1, 3)),
        "wlinT": chunks(np.asarray(L0_tok_W_lin).T),
        "posT": chunks(pos.T),
        "blin": np.ascontiguousarray(np.asarray(L0_tok_b_lin).reshape(KD, P).T),
        "cls": np.ascontiguousarray(np.asarray(L0_tok_class_token).reshape(KD, P).T),
        "txt_win": np.ascontiguousarray(text_in),
        "rest": np.ascontiguousarray(rest[:RT * P].reshape(RT, P, D).transpose(1, 0, 2).reshape(P, RT * D)),
        "rest_last": np.ascontiguousarray(rest[RT * P:]),
        "wq": chunks(L0_attn_Wq), "wk": chunks(L0_attn_Wk), "wv": chunks(wv), "wo": chunks(wo),
        "gateT": chunks(np.asarray(L0_ffn_gate_w).T),
        "expT": chunks(np.asarray(L0_ffn_expert_w).transpose(2, 0, 1).reshape(D, NE * D)),
        "consts": consts,
    }
    outs = {"out_win": (P, PAIRS * D), "out_rest": (P, RT * D), "out_rest_last": (RLAST, D)}
    nc = bacc.Bacc("TRN2", target_bir_lowering=False, num_devices=1)
    args = [nc.dram_tensor(n, a.shape, F32, kind="ExternalInput").ap() for n, a in ins.items()]
    args += [nc.dram_tensor(n, s, F32, kind="ExternalOutput").ap() for n, s in outs.items()]
    fusion_kernel(nc, *args)
    got = run_bass_kernel_spmd(nc, [ins], core_ids=[0]).results[0]

    w = got["out_win"].reshape(2, WIN, PAIRS, D).transpose(2, 0, 1, 3).reshape(B, WIN, D)
    r = np.concatenate([got["out_rest"].reshape(P, RT, D).transpose(1, 0, 2).reshape(RT * P, D),
                        got["out_rest_last"]]).reshape(B, S - WIN, D)
    return np.concatenate([w[:, NPATCH:NPATCH + 1], w[:, :NPATCH], w[:, NPATCH + 1:], r], axis=1)
```

```python
from contextlib import ExitStack

import concourse.bass as bass
from concourse import mybir

F32 = mybir.dt.float32
F32R = mybir.dt.float32r
F16 = mybir.dt.float16
BF16 = mybir.dt.bfloat16
U32 = mybir.dt.uint32
ALU = mybir.AluOpType
ACT = mybir.ActivationFunctionType
AX_X = mybir.AxisListType.X

P = 128
D = 256
KD = D // P
B = 32
S = 114
WIN = 64
NPATCH = 36
FEAT = 768
KF = FEAT // P
HEADS = 16
DH = D // HEADS
NE = 8
GB = 4
PAIRS = B // 2
NG = B // GB
NREST = B * (S - WIN)
RT = NREST // P
RLAST = NREST - RT * P
CH = NE * D // 512
TXT_WIN = WIN - NPATCH - 1
EPS = 1e-5


def fusion_kernel(nc, xT, wlinT, embT, txt_win, rest, rest_last, wqkvo, gateT, expT, consts,
                  out_win, out_rest, out_rest_last):
    ctx = ExitStack()
    with ctx:
        def sb(name, shape, dt=F32):
            return ctx.enter_context(nc.sbuf_tensor(name, shape, dt))

        def bank(name, shape):
            return ctx.enter_context(nc.psum_tensor(name, shape, F32))

        def sem(name):
            return ctx.enter_context(nc.semaphore(name))

        const = sb("const", [P, P + 4 + NE])
        ident = const[:, 0:P]
        head_mask = const[:, P:P + 4]
        iota_e = const[:, P + 4:P + 4 + NE]
        eps_col = sb("eps_col", [P, 4])
        wlin = sb("wlin", [P, KF, D])
        emb_add = sb("emb_add", [P, KD, NPATCH + 3])
        patch_add = sb("patch_add", [P, KD, NPATCH])
        w_raw = sb("w_raw", [P, 4, KD, D])
        w_hi = sb("w_hi", [P, 4, KD, D], F32R)
        w_lo = sb("w_lo", [P, 4, KD, D], F32R)
        g_raw = sb("g_raw", [P, KD, NE])
        g_split = sb("g_split", [P, KD, NE, 2], F32R)
        e_raw = sb("e_raw", [P, KD, NE * D])
        e_hi = sb("e_hi", [P, KD, NE * D], F32R)
        e_lo = sb("e_lo", [P, KD, NE * D], F32R)

        win = sb("win", [P, PAIRS * D])
        rst = sb("rst", [P, (RT + 1) * D])

        xg = sb("xg", [P, KF, GB * NPATCH])
        hT = sb("hT", [P, KD, GB, WIN])
        norm_1 = sb("norm_1", [P, 2, D])
        x1_hi = sb("x1_hi", [P, KD, 2 * P], F32R)
        x1_lo = sb("x1_lo", [P, KD, 2 * P], F32R)
        q_bd = sb("q_bd", [P, KD, GB, 2, WIN])
        k_bd = sb("k_bd", [P, KD, GB, 4, WIN])
        q_hi = sb("q_hi", [P, KD, GB, 2, WIN], F32R)
        q_lo = sb("q_lo", [P, KD, GB, 2, WIN], F32R)
        k_hi = sb("k_hi", [P, KD, GB, 4, WIN], F32R)
        k_lo = sb("k_lo", [P, KD, GB, 4, WIN], F32R)
        v_bd = [sb(f"v_bd{n}", [P, 2 * 8, 2, 32], BF16) for n in range(3)]
        v_rest = sb("v_rest", [P, 2 * 8, 32])

        neg_max = sb("neg_max", [P, 2, 8])
        prob = sb("prob", [P, 8, 2, WIN])
        ssum = sb("ssum", [P, 8, 2])
        sinv = sb("sinv", [P, 8, 2])
        pT_hi = sb("pT_hi", [P, 8, P], F16)
        pT_lo = sb("pT_lo", [P, 8, P], F16)
        attn = sb("attn", [P, 2, 8, DH])
        cT_hi = sb("cT_hi", [P, 2, 2, WIN], F32R)
        cT_lo = sb("cT_lo", [P, 2, 2, WIN], F32R)

        norm_2 = sb("norm_2", [P, 3, D])
        x2_hi = sb("x2_hi", [P, 3, KD, P], F32R)
        x2_lo = sb("x2_lo", [P, 3, KD, P], F32R)
        logit = sb("logit", [P, 3, NE])
        top8 = sb("top8", [P, 3, 8])
        topi = sb("topi", [P, 3, 8], U32)
        topf = sb("topf", [P, 3, 2])
        wexp = sb("wexp", [P, 3, 4])
        wsel = sb("wsel", [P, 3, 2, NE])
        wfull = sb("wfull", [P, 3, NE])

        ST1, STW = RT + 1, RT + 3
        NST = RT + 5
        bn = sb("bn", [P, NST, 6])
        mv = sb("mv", [P, NST, 2])
        ve = sb("ve", [P, NST])
        rstd = sb("rstd", [P, NST])
        negm = sb("negm", [P, NST])
        shift = sb("shift", [P, NST])

        SP_ = bank("score_bank", [P, 2, 512])
        O_ = bank("value_bank", [P, 8, 2, 2, DH])
        T_ = bank("norm_t_bank", [P, KD, P])
        U_ = bank("small_bank", [P, 512])
        PR = bank("proj_bank", [P, 512])
        XB = [bank(f"expert_bank{n}", [P, 512]) for n in range(2)]

        names = """
            d_const d_wlin0 d_wlin1 d_embc d_x d_txt0 d_txt d_rest0 d_rest d_attwqk d_attwvo d_gate
            d_exp0 d_exp1 d_exp2 d_exp3 d_out
            zeroed consts_ready patch_const rest_pad
            attw_hi attw_lo gate_hi gate_lo exp_hi exp_lo_dve exp_lo_pool
            emb_done emb_added hT_done win_added
            bn1 mv1 rstd1_ve rstd1_pow rstd1 bnw mvw rstdw_ve rstdw_pow rstdw
            bnr mvr rstdr_ve rstdr_pow rstdr
            norm1_ready x1T_done x1_hi_done x1_lo_done norm2_ready x2T_done x2_hi_done x2_lo_done
            q_done q_taken q_hi_done q_lo_done k_done k_taken k_hi_done k_lo0_done k_lo_done
            v_done v1_taken vr_ready v2_ready v3_ready
            score_done max_done exp_done inv_done pT_done pT_hi_done pT_lo_done pv_done attn_ready
            cT_done cT_hi_done cT_lo_done wo_done res_done
            logit_done logit_taken top_val index_done ex_done den_done index_float
            weight0_done weight1_done placed_done weights_ready
            chunk_done chunk_part chunk_used"""
        m = {n: sem(n) for n in names.split()}

        def wait(eng, name, value):
            if not (isinstance(value, int) and value <= 0):
                eng.wait_ge(m[name], value)

        def wait_apart(eng, name, value):
            if not isinstance(value, int):
                eng.wait_ge(m["consts_ready"], 1)
            wait(eng, name, value)

        def win_at(t):
            return win[:, bass.ds(t * D, D)]

        def rst_at(r):
            return rst[:, bass.ds(r * D, D)]

        def tile_no(s, slot):
            return 3 * s + 1 + slot

        def rest_of(s):
            return 1 if is_at(s, 0) else s + 3

        BATCH = (0, 2, 5, RT + 1)

        def pair(buf, j):
            return buf[:, :, 2 * j:2 * j + 2].rearrange("p c b h n -> p c (b h n)")

        def bank_part(e, c):
            return e[:, :, 512 * c:512 * (c + 1)]

        def is_at(s, n):
            return isinstance(s, int) and s == n

        def first(s):
            return is_at(s, 0)

        def supersteps(eng, body):
            body(0)
            with eng.Fori(1, NG - 1) as s:
                body(s)

        S_LAST, S_AFTER = NG - 1, NG
        T_A, T_B = 2 * S_LAST, 2 * S_LAST + 1
        X = [tile_no(S_LAST, n) for n in range(3)]
        Y = [tile_no(S_AFTER, n) for n in range(3)]
        Z = tile_no(S_AFTER + 1, 0)

        block = ctx.enter_context(nc.Block())

        @block.sync
        def _(sp):
            sp.dma_start(xg[:], xT[0]).then_inc(m["d_x"], 16)
            for c in range(KD):
                sp.dma_start(wlin[:, :, P * c:P * (c + 1)],
                             wlinT[:, :, P * c:P * (c + 1)]).then_inc(m[f"d_wlin{c}"], 16)
            sp.wait_ge(m["zeroed"], 1)
            for cols, name in ((slice(0, 2 * D), "d_txt0"), (slice(2 * D, PAIRS * D), "d_txt")):
                for b in range(2):
                    sp.dma_start(win[WIN * b + NPATCH + 1:WIN * (b + 1), cols],
                                 txt_win[b, :, cols]).then_inc(m[name], 16)
                if name == "d_txt0":
                    for c in range(CH):
                        sp.dma_start(bank_part(e_raw, c), bank_part(expT, c)).then_inc(m[f"d_exp{c}"], 16)
                        if c == 1:
                            sp.dma_start(w_raw[:, 2:4], wqkvo[:, 2:4]).then_inc(m["d_attwvo"], 16)
                    sp.dma_start(rst[:, BATCH[1] * D:RT * D],
                                 rest[:, BATCH[1] * D:RT * D]).then_inc(m["d_rest"], 16)
            sp.dma_start(rst[0:RLAST, RT * D:(RT + 1) * D], rest_last).then_inc(m["d_rest"], 16)

            def load_patches(s):
                wait(sp, "emb_done", s + 2)
                sp.dma_start(xg[:], xT[s + 2] if isinstance(s, int) else
                             xT[bass.ds(s + 2, 1)].squeeze(0)).then_inc(m["d_x"], 16)

            def store_rest(x, r):
                wait(sp, "chunk_used", CH * (x + 1))
                sp.dma_start(out_rest[:, bass.ds(r * D, D)], rst_at(r)).then_inc(m["d_out"], 16)

            def store_win(x, t):
                wait(sp, "chunk_used", CH * (x + 1))
                sp.dma_start(out_win[:, bass.ds(t * D, D)], win_at(t)).then_inc(m["d_out"], 16)

            wait(sp, "emb_done", 1)
            sp.dma_start(xg[:], xT[1]).then_inc(m["d_x"], 16)

            def superstep(s):
                if not (isinstance(s, int) and s >= NG - 2):
                    load_patches(s)
                store_rest(tile_no(s, 0), rest_of(s))
                for n in (1, 2):
                    if first(s):
                        store_rest(tile_no(s, n), 1 + n)
                    else:
                        store_win(tile_no(s, n), 2 * s - 3 + n)

            store_rest(0, 0)
            superstep(0)
            with sp.Fori(1, NG - 2) as s:
                superstep(s)
            for s in (NG - 2, S_LAST, S_AFTER):
                superstep(s)
            wait(sp, "chunk_used", CH * (tile_no(NG + 1, 0) + 1))
            sp.dma_start(out_rest_last, rst[0:RLAST, RT * D:(RT + 1) * D]).then_inc(m["d_out"], 16)
            sp.wait_ge(m["d_out"], 16 * (PAIRS + RT + 1))

        @block.gpsimd
        def _(pool):
            pool.memset(win[:], 0.0).then_inc(m["zeroed"], 1)
            pool.memset(hT[:], 0.0).then_inc(m["zeroed"], 1)
            pool.memset(eps_col[:, 0:1], EPS)
            pool.memset(eps_col[:, 1:2], -0.5)
            pool.memset(eps_col[:, 3:4], -1.0)
            pool.memset(eps_col[:, 2:3], 1.0).then_inc(m["consts_ready"], 1)
            pool.wait_ge(m["consts_ready"], 1)

            def inverse_deviation(kind, n, c):
                wait(pool, {"rstd1": "mv1", "rstdw": "mvw"}[kind], n + 1)
                pool.tensor_tensor(ve[:, c:c + 1], mv[:, c, 1:2], eps_col[:, 0:1],
                                   ALU.add).then_inc(m[kind + "_ve"], 1)
                wait(pool, kind + "_ve", n + 1)
                pool.tensor_tensor(rstd[:, c:c + 1], ve[:, c:c + 1], eps_col[:, 1:2],
                                   ALU.pow).then_inc(m[kind + "_pow"], 1)
                wait_apart(pool, kind + "_pow", n + 1)
                pool.tensor_scalar(shift[:, c:c + 1], mv[:, c, 0:1], -1.0,
                                   rstd[:, c:c + 1], ALU.mult, ALU.mult).then_inc(m[kind], 1)

            def inverse_deviation_rest(n):
                r0, r1 = BATCH[n], BATCH[n + 1]
                r = slice(r0, r1)

                def column(c):
                    return eps_col[:, c:c + 1].to_broadcast([P, r1 - r0])
                pool.wait_ge(m["mvr"], r1)
                pool.tensor_tensor(ve[:, r], mv[:, r, 1], column(0), ALU.add).then_inc(m["rstdr_ve"], 1)
                pool.tensor_tensor(negm[:, r], mv[:, r, 0], column(3), ALU.mult).then_inc(m["rstdr_ve"], 1)
                pool.wait_ge(m["rstdr_ve"], 2 * (n + 1))
                pool.tensor_tensor(rstd[:, r], ve[:, r], column(1), ALU.pow).then_inc(m["rstdr_pow"], 1)
                pool.wait_ge(m["rstdr_pow"], n + 1)
                pool.tensor_tensor(shift[:, r], negm[:, r], rstd[:, r], ALU.mult).then_inc(m["rstdr"], 1)

            def gate(x, slot):
                e, den, w0, w1 = (wexp[:, slot, n:n + 1] for n in range(4))
                wait(pool, "ex_done", x + 1)
                pool.tensor_tensor(den, e, eps_col[:, 2:3], ALU.add).then_inc(m["den_done"], 1)
                wait_apart(pool, "index_done", x + 1)
                pool.tensor_copy(topf[:, slot], topi[:, slot, 0:2]).then_inc(m["index_float"], 1)
                wait(pool, "den_done", x + 1)
                pool.tensor_tensor(w0, den, eps_col[:, 3:4], ALU.pow).then_inc(m["weight0_done"], 1)
                wait(pool, "weight0_done", x + 1)
                pool.tensor_tensor(w1, e, w0, ALU.mult).then_inc(m["weight1_done"], 1)
                wait_apart(pool, "weight1_done", x + 1)
                wait(pool, "index_float", x + 1)
                for n, w in enumerate((w0, w1)):
                    pool.tensor_scalar(wsel[:, slot, n], iota_e[:], topf[:, slot, n:n + 1], w,
                                       ALU.is_equal, ALU.mult).then_inc(m["placed_done"], 1)
                wait(pool, "placed_done", 2 * (x + 1))
                pool.tensor_tensor(wfull[:, slot], wsel[:, slot, 0], wsel[:, slot, 1],
                                   ALU.add).then_inc(m["weights_ready"], 1)

            def q_lo_part(g, j):
                wait(pool, "q_hi_done", 2 * g + j + 1)
                pool.tensor_tensor(pair(q_lo, j), pair(q_bd, j), pair(q_hi, j).bitcast(F32),
                                   ALU.subtract).then_inc(m["q_lo_done"], 1)

            def k_lo_part(g, j):
                wait(pool, "k_hi_done", 2 * g + j + 1)
                pool.tensor_tensor(pair(k_lo, j), pair(k_bd, j), pair(k_hi, j).bitcast(F32),
                                   ALU.subtract).then_inc(m["k_lo_done"], 1)

            def last_v_part(g, before, count):
                wait(pool, before, count)
                wait(pool, "v2_ready", 2 * (g + 1))
                wait(pool, "vr_ready", 2 * (g + 1))
                for b in range(2):
                    h = slice(WIN * b, WIN * (b + 1))
                    pool.tensor_tensor(v_bd[2][h, :, b], v_rest[h], v_bd[1][h, :, b],
                                       ALU.subtract).then_inc(m["v3_ready"], 1)
                    wait(pool, "v3_ready", 2 * g + b + 1)

            pool.wait_ge(m["d_const"], 16)
            inverse_deviation_rest(0)
            inverse_deviation("rstd1", 0, ST1)
            inverse_deviation("rstd1", 1, ST1 + 1)

            def split_experts(c):
                pool.wait_ge(m["exp_hi"], c + 1)
                for k in range(KD):
                    w = slice(512 * c, 512 * (c + 1))
                    pool.tensor_tensor(e_lo[:, k, w], e_raw[:, k, w], e_hi[:, k, w].bitcast(F32),
                                       ALU.subtract).then_inc(m["exp_lo_pool"], 1)

            split_experts(1)
            gate(0, 2)
            split_experts(3)
            q_lo_part(0, 0)
            inverse_deviation_rest(1)
            gate(1, 0)
            pool.wait_ge(m["patch_const"], 1)
            last_v_part(0, "rstdr", 2)
            q_lo_part(0, 1)
            k_lo_part(0, 1)

            def superstep(s):
                gate(tile_no(s, 1), 1)
                inverse_deviation("rstd1", 2 * (s + 1), ST1)
                inverse_deviation("rstd1", 2 * (s + 1) + 1, ST1 + 1)
                inverse_deviation("rstdw", 2 * s, STW)
                gate(tile_no(s, 2), 2)
                q_lo_part(s + 1, 0)
                k_lo_part(s + 1, 0)
                gate(tile_no(s + 1, 0), 0)
                if first(s):
                    inverse_deviation_rest(2)
                inverse_deviation("rstdw", 2 * s + 1, STW + 1)
                last_v_part(s + 1, "rstdw", 2 * s + 2)
                q_lo_part(s + 1, 1)
                k_lo_part(s + 1, 1)

            supersteps(pool, superstep)
            gate(X[1], 1)
            gate(X[2], 2)
            inverse_deviation("rstdw", T_A, STW)
            gate(Y[0], 0)
            gate(Y[1], 1)
            inverse_deviation("rstdw", T_B, STW + 1)
            gate(Y[2], 2)
            gate(Z, 0)

        @block.scalar
        def _(act):
            act.dma_start(const[:], consts).then_inc(m["d_const"], 16)
            act.dma_start(emb_add[:], embT).then_inc(m["d_embc"], 16)
            act.dma_start(rst[:, 0:BATCH[1] * D], rest[:, 0:BATCH[1] * D]).then_inc(m["d_rest0"], 16)
            act.dma_start(w_raw[:, 0:2], wqkvo[:, 0:2]).then_inc(m["d_attwqk"], 16)
            act.dma_start(g_raw[:], gateT).then_inc(m["d_gate"], 16)

            def copy(out, in_, **kw):
                return act.activation(out, in_, ACT.Copy, **kw)

            def normalise(out, src, n):
                return act.activation(out, src, ACT.Identity, scale=rstd[:, bass.ds(n, 1)],
                                      bias=shift[:, bass.ds(n, 1)])

            def norm1(g, j):
                wait(act, "rstd1", 2 * g + j + 1)
                normalise(norm_1[:, j], win_at(2 * g + j), ST1 + j).then_inc(m["norm1_ready"], 1)

            def norm2_win(slot, t):
                wait(act, "rstdw", t + 1)
                normalise(norm_2[:, slot], win_at(t), STW + slot - 1).then_inc(m["norm2_ready"], 1)

            def norm2_rest(slot, r):
                wait(act, "rstdr", sum(r >= n for n in BATCH[:-1]) if isinstance(r, int) else len(BATCH) - 1)
                normalise(norm_2[:, slot], rst_at(r), r).then_inc(m["norm2_ready"], 1)

            def norm2_hi(x, slot):
                wait(act, "x2T_done", x + 1)
                copy(x2_hi[:, slot], T_[:]).then_inc(m["x2_hi_done"], 1)

            def gate_exp(x, slot):
                wait(act, "top_val", x + 1)
                act.activation(wexp[:, slot, 0:1], top8[:, slot, 0:1], ACT.Exp, scale=-1.0,
                               bias=top8[:, slot, 1:2]).then_inc(m["ex_done"], 1)

            def softmax_exp(t, b):
                wait(act, "max_done", 2 * t + b + 1)
                for c in range(8):
                    i = act.activation(prob[:, c, b], SP_[:, b, WIN * c:WIN * (c + 1)], ACT.Exp,
                                       bias=neg_max[:, b, c:c + 1], accum_out=ssum[:, c, b:b + 1])
                if b == 1:
                    i.then_inc(m["exp_done"], 1)

            def prob_hi(t):
                wait(act, "pT_done", t + 1)
                copy(pT_hi[:].rearrange("p c q -> p (c q)"),
                     SP_[:].rearrange("p b n -> p (b n)")).then_inc(m["pT_hi_done"], 1)

            def context_hi(t):
                wait(act, "cT_done", t + 1)
                copy(cT_hi[:].rearrange("p h b q -> p b h q"),
                     U_[:, 0:D].rearrange("p (b h q) -> p b h q", b=2, h=2)).then_inc(m["cT_hi_done"], 1)

            def norm1_hi(g, j):
                wait(act, "x1T_done", 2 * g + j + 1)
                copy(x1_hi[:, :, P * j:P * (j + 1)], T_[:]).then_inc(m["x1_hi_done"], 1)

            def take_q(g):
                wait(act, "q_done", g + 1)
                if first(g):
                    act.wait_ge(m["patch_const"], 1)
                src = PR[:].rearrange("p (n q) -> p n q", q=WIN)
                for hs in range(2):
                    h = slice(WIN * hs, WIN * (hs + 1))
                    copy(q_bd[h].rearrange("p c b h q -> p (c b) h q")[:, :, hs], src[h],
                         scale=DH ** -0.5).then_inc(m["q_taken"], 1)

            def take_k(g):
                wait(act, "k_done", g + 1)
                src = PR[:].rearrange("p (n q) -> p n q", q=WIN)
                for hh in range(4):
                    copy(k_bd[:].rearrange("p c b h k -> p (c b) h k")[:, :, hh], src,
                         scale=head_mask[:, hh:hh + 1]).then_inc(m["k_taken"], 1)

            def q_hi_part(g, j):
                wait(act, "q_taken", 2 * (g + 1))
                copy(pair(q_hi, j), pair(q_bd, j)).then_inc(m["q_hi_done"], 1)

            def k_hi_part(g, j):
                wait(act, "k_taken", 4 * (g + 1))
                copy(pair(k_hi, j), pair(k_bd, j)).then_inc(m["k_hi_done"], 1)

            def take_v(g):
                wait(act, "v_done", g + 1)
                src = PR[:].rearrange("p (n d) -> p n d", d=32)
                for b in range(2):
                    h = slice(WIN * b, WIN * (b + 1))
                    copy(v_bd[0][h, :, b], src[h]).then_inc(m["v1_taken"], 1)

            def second_v_part(g):
                wait(act, "vr_ready", 2 * (g + 1))
                for b in range(2):
                    h = slice(WIN * b, WIN * (b + 1))
                    copy(v_bd[1][h, :, b], v_rest[h]).then_inc(m["v2_ready"], 1)

            norm2_rest(2, 0)
            norm2_rest(0, 1)
            act.wait_ge(m["d_attwqk"], 16)
            copy(w_hi[:, 0:2].rearrange("p a b c -> p (a b c)"),
                 w_raw[:, 0:2].rearrange("p a b c -> p (a b c)")).then_inc(m["attw_hi"], 1)
            act.wait_ge(m["d_const"], 16)
            norm2_hi(0, 2)
            act.wait_ge(m["d_gate"], 16)
            copy(g_split[:, :, :, 0], g_raw[:]).then_inc(m["gate_hi"], 1)

            def split_experts(c):
                act.wait_ge(m[f"d_exp{c}"], 16)
                copy(bank_part(e_hi, c), bank_part(e_raw, c)).then_inc(m["exp_hi"], 1)

            split_experts(0)
            split_experts(1)
            norm1(0, 0)
            norm1(0, 1)
            norm1_hi(0, 0)
            act.wait_ge(m["d_attwvo"], 16)
            copy(w_hi[:, 2:4].rearrange("p a b c -> p (a b c)"),
                 w_raw[:, 2:4].rearrange("p a b c -> p (a b c)")).then_inc(m["attw_hi"], 1)
            norm1_hi(0, 1)
            split_experts(2)
            gate_exp(0, 2)
            split_experts(3)
            norm2_hi(1, 0)
            take_q(0)
            q_hi_part(0, 0)
            take_k(0)
            k_hi_part(0, 0)
            gate_exp(1, 0)
            norm2_rest(1, 2)
            take_v(0)
            second_v_part(0)
            q_hi_part(0, 1)
            k_hi_part(0, 1)

            def superstep(s):
                norm2_hi(tile_no(s, 1), 1)
                softmax_exp(2 * s, 0)
                softmax_exp(2 * s, 1)
                gate_exp(tile_no(s, 1), 1)
                prob_hi(2 * s)
                norm1(s + 1, 0)
                if first(s):
                    norm2_rest(2, 3)
                else:
                    norm2_win(2, 2 * s - 1)
                norm1_hi(s + 1, 0)
                norm1(s + 1, 1)
                norm1_hi(s + 1, 1)
                softmax_exp(2 * s + 1, 0)
                context_hi(2 * s)
                softmax_exp(2 * s + 1, 1)
                norm2_hi(tile_no(s, 2), 2)
                take_q(s + 1)
                norm2_rest(0, rest_of(s + 1))
                prob_hi(2 * s + 1)
                gate_exp(tile_no(s, 2), 2)
                q_hi_part(s + 1, 0)
                take_k(s + 1)
                norm2_hi(tile_no(s + 1, 0), 0)
                k_hi_part(s + 1, 0)
                take_v(s + 1)
                norm2_win(1, 2 * s)
                gate_exp(tile_no(s + 1, 0), 0)
                context_hi(2 * s + 1)
                second_v_part(s + 1)
                q_hi_part(s + 1, 1)
                k_hi_part(s + 1, 1)

            supersteps(act, superstep)

            norm2_hi(X[1], 1)
            softmax_exp(T_A, 0)
            softmax_exp(T_A, 1)
            norm2_win(2, T_A - 1)
            gate_exp(X[1], 1)
            prob_hi(T_A)
            norm2_hi(X[2], 2)
            norm2_rest(0, rest_of(S_AFTER))
            norm2_hi(Y[0], 0)
            softmax_exp(T_B, 0)
            gate_exp(X[2], 2)
            context_hi(T_A)
            softmax_exp(T_B, 1)
            prob_hi(T_B)
            norm2_win(1, T_A)
            norm2_hi(Y[1], 1)
            gate_exp(Y[0], 0)
            gate_exp(Y[1], 1)
            context_hi(T_B)
            norm2_win(2, T_B)
            norm2_rest(0, RT)
            norm2_hi(Y[2], 2)
            gate_exp(Y[2], 2)
            norm2_hi(Z, 0)
            gate_exp(Z, 0)

        @block.vector
        def _(dve):
            def stats(kind, n, slot, src):
                bn_sem, mv_sem = {"1": ("bn1", "mv1"), "w": ("bnw", "mvw"), "r": ("bnr", "mvr")}[kind]
                dve.bn_stats(bn[:, slot], src).then_inc(m[bn_sem], 1)
                wait_apart(dve, bn_sem, n + 1)
                dve.bn_aggr(mv[:, slot], bn[:, slot]).then_inc(m[mv_sem], 1)

            def rest_stats(*tiles):
                for r in tiles:
                    stats("r", r, r, rst_at(r))

            def norm2_lo(x, slot):
                wait(dve, "x2_hi_done", x + 1)
                dve.tensor_tensor(x2_lo[:, slot], T_[:],
                                  x2_hi[:, slot].bitcast(F32), ALU.subtract).then_inc(m["x2_lo_done"], 1)

            def top_two(x, slot):
                wait(dve, "logit_done", x + 1)
                lg = logit[:, slot]
                dve.reduce_sum(lg, U_[:, 0:2 * NE].rearrange("p (e n) -> p e n", n=2),
                               AX_X).then_inc(m["logit_taken"], 1)
                wait_apart(dve, "logit_taken", x + 1)
                dve.max(top8[:, slot], lg).then_inc(m["top_val"], 1)
                wait_apart(dve, "top_val", x + 1)
                dve.max_index(topi[:, slot], top8[:, slot], lg).then_inc(m["index_done"], 1)

            def experts(x, slot, c, acc):
                if c == 0:
                    wait(dve, "weights_ready", x + 1)
                else:
                    wait(dve, "chunk_used", CH * x + c)
                wait(dve, "chunk_done", CH * x + c + 1)
                for n in range(2):
                    e = 2 * c + n
                    i = dve.scalar_tensor_tensor(out=acc, in0=XB[c % 2][:, D * n:D * (n + 1)],
                                                 scalar=wfull[:, slot, e:e + 1], in1=acc,
                                                 op0=ALU.mult, op1=ALU.add)
                    if n == 0:
                        i.then_inc(m["chunk_part"], 1)
                        wait(dve, "chunk_part", CH * x + c + 1)
                i.then_inc(m["chunk_used"], 1)

            def take_embedding(g):
                wait(dve, "emb_done", g + 1)
                src = PR[:, 0:KD * GB * NPATCH].rearrange("p (c b n) -> p c b n", c=KD, b=GB)
                dve.tensor_tensor(hT[:, :, :, 0:NPATCH], src,
                                  patch_add[:].unsqueeze(2).to_broadcast([P, KD, GB, NPATCH]),
                                  ALU.add).then_inc(m["emb_added"], 1)

            def add_window(g, j):
                t = 2 * g + j
                wait(dve, "hT_done", t + 1)
                dve.tensor_tensor(win_at(t), U_[:, 0:D], win_at(t), ALU.add).then_inc(m["win_added"], 1)

            def window_stats(g, j):
                t = 2 * g + j
                wait_apart(dve, "win_added", t + 1)
                stats("1", t, ST1 + j, win_at(t))

            def norm1_lo(g, j):
                wait(dve, "x1_hi_done", 2 * g + j + 1)
                c = slice(P * j, P * (j + 1))
                dve.tensor_tensor(x1_lo[:, :, c], T_[:], x1_hi[:, :, c].bitcast(F32),
                                  ALU.subtract).then_inc(m["x1_lo_done"], 1)

            def softmax_max(t):
                for b in range(2):
                    wait(dve, "score_done", 2 * t + b + 1)
                    dve.tensor_reduce(neg_max[:, b], SP_[:, b].rearrange("p (c k) -> p c k", k=WIN), AX_X,
                                      ALU.max, negate=True).then_inc(m["max_done"], 1)

            def softmax_inverse(t):
                wait(dve, "exp_done", t + 1)
                dve.reciprocal(sinv[:], ssum[:]).then_inc(m["inv_done"], 1)

            def prob_lo(t):
                wait(dve, "pT_hi_done", t + 1)
                dve.tensor_tensor(pT_lo[:].rearrange("p c q -> p (c q)"), SP_[:].rearrange("p b n -> p (b n)"),
                                  pT_hi[:].rearrange("p c q -> p (c q)"),
                                  ALU.subtract).then_inc(m["pT_lo_done"], 1)

            def take_context(t):
                wait(dve, "pv_done", t + 1)
                wait(dve, "inv_done", t + 1)
                for hs in range(2):
                    h = slice(WIN * hs, WIN * (hs + 1))
                    dve.tensor_tensor(attn[h].rearrange("p b c d -> p c b d"), O_[h, :, :, hs],
                                      sinv[h].unsqueeze(3)
                                      .to_broadcast([WIN, 8, 2, DH]), ALU.mult).then_inc(m["attn_ready"], 1)

            def context_lo(t):
                wait(dve, "cT_hi_done", t + 1)
                dve.tensor_tensor(cT_lo[:].rearrange("p h b q -> p b h q"),
                                  U_[:, 0:D].rearrange("p (b h q) -> p b h q", b=2, h=2),
                                  cT_hi[:].rearrange("p h b q -> p b h q").bitcast(F32),
                                  ALU.subtract).then_inc(m["cT_lo_done"], 1)

            def add_attention(s, j):
                t = 2 * s + j
                wait(dve, "wo_done", t + 1)
                dve.tensor_tensor(win_at(t), U_[:, 0:D], win_at(t), ALU.add).then_inc(m["res_done"], 1)
                wait_apart(dve, "res_done", t + 1)
                stats("w", t, STW + j, win_at(t))

            def v_minus_first(g):
                wait(dve, "v1_taken", 2 * (g + 1))
                src = PR[:].rearrange("p (n d) -> p n d", d=32)
                for b in range(2):
                    h = slice(WIN * b, WIN * (b + 1))
                    dve.tensor_tensor(v_rest[h], src[h], v_bd[0][h, :, b], ALU.subtract).then_inc(m["vr_ready"], 1)

            pad = slice(RLAST, P)
            dve.memset(rst[pad, RT * D:(RT + 1) * D], 0.0).then_inc(m["rest_pad"], 1)
            dve.memset(q_bd[:], 0.0)
            for n in range(3):
                dve.memset(v_bd[n][:], 0.0)
            dve.wait_ge(m["d_embc"], 16)
            for c in range(KD):
                dve.tensor_scalar(patch_add[:, c], emb_add[:, c, 1:NPATCH + 1],
                                  emb_add[:, c, NPATCH + 1:NPATCH + 2], None, ALU.add)
            dve.wait_ge(m["zeroed"], 2)
            dve.tensor_tensor(hT[:, :, :, NPATCH:NPATCH + 1],
                              emb_add[:, :, 0:1].unsqueeze(2).to_broadcast([P, KD, GB, 1]),
                              emb_add[:, :, NPATCH + 2:].unsqueeze(2).to_broadcast([P, KD, GB, 1]),
                              ALU.add).then_inc(m["patch_const"], 1)
            dve.wait_ge(m["d_rest0"], 16)
            rest_stats(0, 1)
            dve.wait_ge(m["patch_const"], 1)
            take_embedding(0)
            dve.wait_ge(m["d_txt0"], 32)
            for j in range(2):
                add_window(0, j)
                window_stats(0, j)
            norm2_lo(0, 2)

            def split_weights(n):
                w = slice(2 * n, 2 * n + 2)
                dve.wait_ge(m["attw_hi"], n + 1)
                dve.tensor_tensor(w_lo[:, w].rearrange("p a b c -> p (a b c)"),
                                  w_raw[:, w].rearrange("p a b c -> p (a b c)"),
                                  w_hi[:, w].rearrange("p a b c -> p (a b c)").bitcast(F32),
                                  ALU.subtract).then_inc(m["attw_lo"], 1)

            split_weights(0)
            dve.wait_ge(m["gate_hi"], 1)
            dve.tensor_tensor(g_split[:, :, :, 1], g_raw[:], g_split[:, :, :, 0].bitcast(F32),
                              ALU.subtract).then_inc(m["gate_lo"], 1)

            def split_experts(c):
                dve.wait_ge(m["exp_hi"], c + 1)
                dve.tensor_tensor(bank_part(e_lo, c), bank_part(e_raw, c), bank_part(e_hi, c).bitcast(F32),
                                  ALU.subtract).then_inc(m["exp_lo_dve"], 1)

            norm1_lo(0, 0)
            split_experts(0)
            norm1_lo(0, 1)
            top_two(0, 2)
            split_weights(1)
            split_experts(2)
            norm2_lo(1, 0)
            experts(0, 2, 0, rst_at(0))
            experts(0, 2, 1, rst_at(0))
            dve.wait_ge(m["d_rest"], 32)
            dve.wait_ge(m["rest_pad"], 1)
            rest_stats(2, 3, 4)
            top_two(1, 0)
            experts(0, 2, 2, rst_at(0))
            experts(0, 2, 3, rst_at(0))
            dve.wait_ge(m["k_hi_done"], 1)
            dve.tensor_tensor(pair(k_lo, 0), pair(k_bd, 0), pair(k_hi, 0).bitcast(F32),
                              ALU.subtract).then_inc(m["k_lo0_done"], 1)
            v_minus_first(0)
            rest_stats(5, 6, 7)
            dve.wait_ge(m["d_txt"], 32)

            def superstep(s):
                x = [tile_no(s, n) for n in range(3)]
                acc = [rst_at(rest_of(s))] + [rst_at(2 + n) if first(s) else win_at(2 * s - 2 + n)
                                              for n in range(2)]
                softmax_max(2 * s)
                norm2_lo(x[1], 1)
                take_embedding(s + 1)
                experts(x[0], 0, 0, acc[0])
                top_two(x[1], 1)
                add_window(s + 1, 0)
                experts(x[0], 0, 1, acc[0])
                window_stats(s + 1, 0)
                experts(x[0], 0, 2, acc[0])
                add_window(s + 1, 1)
                prob_lo(2 * s)
                window_stats(s + 1, 1)
                softmax_inverse(2 * s)
                experts(x[0], 0, 3, acc[0])
                norm1_lo(s + 1, 0)
                experts(x[1], 1, 0, acc[1])
                take_context(2 * s)
                softmax_max(2 * s + 1)
                norm1_lo(s + 1, 1)
                experts(x[1], 1, 1, acc[1])
                context_lo(2 * s)
                experts(x[1], 1, 2, acc[1])
                if first(s):
                    rest_stats(8, 9)
                norm2_lo(x[2], 2)
                add_attention(s, 0)
                top_two(x[2], 2)
                prob_lo(2 * s + 1)
                experts(x[1], 1, 3, acc[1])
                softmax_inverse(2 * s + 1)
                experts(x[2], 2, 0, acc[2])
                if first(s):
                    rest_stats(10)
                norm2_lo(tile_no(s + 1, 0), 0)
                take_context(2 * s + 1)
                top_two(tile_no(s + 1, 0), 0)
                if first(s):
                    rest_stats(11, 12)
                v_minus_first(s + 1)
                context_lo(2 * s + 1)
                experts(x[2], 2, 1, acc[2])
                experts(x[2], 2, 2, acc[2])
                add_attention(s, 1)
                experts(x[2], 2, 3, acc[2])

            supersteps(dve, superstep)

            acc = [rst_at(rest_of(S_LAST)), win_at(T_A - 2), win_at(T_A - 1)]
            softmax_max(T_A)
            norm2_lo(X[1], 1)
            experts(X[0], 0, 0, acc[0])
            experts(X[0], 0, 1, acc[0])
            top_two(X[1], 1)
            experts(X[0], 0, 2, acc[0])
            experts(X[0], 0, 3, acc[0])
            prob_lo(T_A)
            norm2_lo(X[2], 2)
            softmax_inverse(T_A)
            experts(X[1], 1, 0, acc[1])
            experts(X[1], 1, 1, acc[1])
            norm2_lo(Y[0], 0)
            softmax_max(T_B)
            take_context(T_A)
            top_two(X[2], 2)
            experts(X[1], 1, 2, acc[1])
            context_lo(T_A)
            experts(X[1], 1, 3, acc[1])
            add_attention(S_LAST, 0)
            experts(X[2], 2, 0, acc[2])
            prob_lo(T_B)
            softmax_inverse(T_B)
            experts(X[2], 2, 1, acc[2])
            top_two(Y[0], 0)
            norm2_lo(Y[1], 1)
            take_context(T_B)
            experts(X[2], 2, 2, acc[2])
            top_two(Y[1], 1)
            experts(X[2], 2, 3, acc[2])
            context_lo(T_B)
            acc = [rst_at(rest_of(S_AFTER)), win_at(T_A), win_at(T_B)]
            experts(Y[0], 0, 0, acc[0])
            add_attention(S_LAST, 1)
            for c in (1, 2, 3):
                experts(Y[0], 0, c, acc[0])
            norm2_lo(Y[2], 2)
            experts(Y[1], 1, 0, acc[1])
            experts(Y[1], 1, 1, acc[1])
            top_two(Y[2], 2)
            norm2_lo(Z, 0)
            experts(Y[1], 1, 2, acc[1])
            experts(Y[1], 1, 3, acc[1])
            top_two(Z, 0)
            for c in range(CH):
                experts(Y[2], 2, c, acc[2])
            for c in range(CH):
                experts(Z, 0, c, rst_at(RT))

        @block.tensor
        def _(pe):
            def split_product(out, terms):
                n = 0
                for (lh, ll), (rh, rl) in terms:
                    for lhs, rhs in ((lh, rh), (lh, rl), (ll, rh)):
                        n += 1
                        i = pe.matmul(out, lhs, rhs, start=(n == 1), stop=(n == 3 * len(terms)))
                return i

            def transpose_norm2(x, slot):
                wait(pe, "norm2_ready", x + 1)
                for k in range(KD):
                    i = pe.transpose(T_[:, k], norm_2[:, slot, P * k:P * (k + 1)], ident)
                i.then_inc(m["x2T_done"], 1)

            def x2(slot, k):
                return x2_hi[:, slot, k], x2_lo[:, slot, k]

            def logits(x, slot):
                wait(pe, "x2_lo_done", x + 1)
                terms = [(part, k) for k in range(KD) for part in x2(slot, k)]
                for n, (part, k) in enumerate(terms):
                    i = pe.matmul(U_[:, 0:2 * NE], part, g_split[:, k].rearrange("p e n -> p (e n)"),
                                  start=(n == 0), stop=(n == len(terms) - 1))
                i.then_inc(m["logit_done"], 1)

            def experts(x, slot, c):
                wait(pe, "chunk_used", CH * x + c - 1)
                w = slice(512 * c, 512 * (c + 1))
                split_product(XB[c % 2][:], [(x2(slot, k), (e_hi[:, k, w], e_lo[:, k, w]))
                                             for k in range(KD)]).then_inc(m["chunk_done"], 1)

            def embed(g):
                wait(pe, "d_x", 16 * (g + 1))
                for c in range(KD):
                    if is_at(g, 0):
                        pe.wait_ge(m[f"d_wlin{c}"], 16)
                    for k in range(KF):
                        i = pe.matmul(PR[:, GB * NPATCH * c:GB * NPATCH * (c + 1)], wlin[:, k, P * c:P * (c + 1)],
                                      xg[:, k], start=(k == 0), stop=(k == KF - 1))
                i.then_inc(m["emb_done"], 1)

            def embed_back(g, j):
                wait(pe, "emb_added", g + 1)
                for c in range(KD):
                    i = pe.transpose(U_[:, P * c:P * (c + 1)],
                                     hT[:, c, 2 * j:2 * j + 2].rearrange("p b n -> p (b n)"), ident)
                i.then_inc(m["hT_done"], 1)

            def transpose_norm1(g, j):
                wait(pe, "norm1_ready", 2 * g + j + 1)
                for k in range(KD):
                    i = pe.transpose(T_[:, k], norm_1[:, j, P * k:P * (k + 1)], ident)
                i.then_inc(m["x1T_done"], 1)

            def w_pair(n, k, cols):
                return w_hi[:, n, k, cols], w_lo[:, n, k, cols]

            def project(g, n, name):
                for c in range(KD):
                    i = split_product(PR[:, 2 * P * c:2 * P * (c + 1)],
                                      [(w_pair(n, k, slice(P * c, P * (c + 1))), (x1_hi[:, k], x1_lo[:, k]))
                                       for k in range(KD)])
                i.then_inc(m[name], 1)

            def project_v(g):
                for j in range(2):
                    c = slice(P * j, P * (j + 1))
                    i = split_product(PR[:, D * j:D * (j + 1)],
                                      [((x1_hi[:, k, c], x1_lo[:, k, c]), w_pair(2, k, slice(0, D)))
                                       for k in range(KD)])
                i.then_inc(m["v_done"], 1)

            def scores(s, j):
                t = 2 * s + j
                wait(pe, "q_lo_done", t + 1)
                if first(t):
                    wait(pe, "k_lo0_done", 1)
                wait(pe, "k_lo_done", t)
                wait(pe, "pT_lo_done", t)
                for b in range(2):
                    for c in range(KD):
                        q = [part[:, c, 2 * j + b].rearrange("p h q -> p (h q)") for part in (q_hi, q_lo)]
                        k = [part[:, c, 2 * j + b].rearrange("p h k -> p (h k)") for part in (k_hi, k_lo)]
                        i = split_product(SP_[:, b, D * c:D * (c + 1)], [(q, k)])
                    i.then_inc(m["score_done"], 1)

            def transpose_prob(t):
                wait(pe, "exp_done", t + 1)
                pt = SP_[:].rearrange("p b (c q) -> p (b c) q", q=P)
                for c in range(8):
                    i = pe.transpose(pt[:, c], prob[:, c].rearrange("p b k -> p (b k)"), ident)
                i.then_inc(m["pT_done"], 1)

            def values(s, j):
                t = 2 * s + j
                wait(pe, "pT_lo_done", t + 1)
                wait(pe, "v3_ready", 2 * (s + 1))
                wait(pe, "attn_ready", 2 * t)
                for c in range(8):
                    terms = [(pT_hi, 0), (pT_hi, 1), (pT_hi, 2), (pT_lo, 0), (pT_lo, 1)]
                    for n, (pr, v) in enumerate(terms):
                        i = pe.matmul(O_[:, c].rearrange("p b h d -> p (b h d)"), pr[:, c],
                                      v_bd[v][:, 8 * j + c].rearrange("p b d -> p (b d)"),
                                      start=(n == 0), stop=(n == len(terms) - 1))
                i.then_inc(m["pv_done"], 1)

            def transpose_context(t):
                wait(pe, "attn_ready", 2 * (t + 1))
                for b in range(2):
                    i = pe.transpose(U_[:, P * b:P * (b + 1)], attn[:, b].rearrange("p c d -> p (c d)"), ident)
                i.then_inc(m["cT_done"], 1)

            def project_out(t):
                wait(pe, "cT_lo_done", t + 1)
                terms = [([part[:, h].rearrange("p b q -> p (b q)") for part in (cT_hi, cT_lo)],
                          w_pair(3, h, slice(0, D))) for h in range(2)]
                split_product(U_[:, 0:D], terms).then_inc(m["wo_done"], 1)

            embed(0)
            pe.wait_ge(m["d_const"], 16)
            transpose_norm2(0, 2)
            for j in range(2):
                wait(pe, "win_added", j)
                embed_back(0, j)
            wait(pe, "x2_lo_done", 1)
            transpose_norm1(0, 0)
            pe.wait_ge(m["gate_lo"], 1)
            wait(pe, "win_added", 2)
            logits(0, 2)
            wait(pe, "x1_lo_done", 1)
            transpose_norm1(0, 1)
            pe.wait_ge(m["exp_lo_dve"], 1)
            experts(0, 2, 0)
            wait(pe, "x1_lo_done", 2)
            transpose_norm2(1, 0)
            pe.wait_ge(m["attw_lo"], 1)
            project(0, 0, "q_done")
            pe.wait_ge(m["exp_lo_pool"], KD)
            experts(0, 2, 1)
            wait(pe, "q_taken", 2)
            project(0, 1, "k_done")
            wait(pe, "logit_taken", 1)
            logits(1, 0)
            pe.wait_ge(m["exp_lo_dve"], 2)
            experts(0, 2, 2)
            pe.wait_ge(m["exp_lo_pool"], 2 * KD)
            experts(0, 2, 3)
            wait(pe, "k_taken", 4)
            pe.wait_ge(m["attw_lo"], 2)
            project_v(0)

            def superstep(s):
                x = [tile_no(s, n) for n in range(3)]
                nx = tile_no(s + 1, 0)
                g = s + 1
                scores(s, 0)
                wait(pe, "x2_lo_done", x[1])
                transpose_norm2(x[1], 1)
                wait(pe, "vr_ready", 2 * g)
                embed(g)
                experts(x[0], 0, 0)
                if first(s):
                    wait(pe, "logit_taken", x[1])
                else:
                    wait(pe, "res_done", 2 * s)
                logits(x[1], 1)
                experts(x[0], 0, 1)
                wait(pe, "logit_taken", x[1] + 1)
                embed_back(g, 0)
                experts(x[0], 0, 2)
                wait(pe, "win_added", 2 * g + 1)
                embed_back(g, 1)
                transpose_prob(2 * s)
                experts(x[0], 0, 3)
                experts(x[1], 1, 0)
                wait(pe, "x2_lo_done", x[1] + 1)
                transpose_norm1(g, 0)
                values(s, 0)
                scores(s, 1)
                wait(pe, "x1_lo_done", 2 * g + 1)
                transpose_norm1(g, 1)
                experts(x[1], 1, 1)
                wait(pe, "win_added", 2 * g + 2)
                transpose_context(2 * s)
                experts(x[1], 1, 2)
                wait(pe, "x1_lo_done", 2 * g + 2)
                transpose_norm2(x[2], 2)
                project(g, 0, "q_done")
                project_out(2 * s)
                experts(x[1], 1, 3)
                transpose_prob(2 * s + 1)
                wait(pe, "res_done", 2 * s + 1)
                logits(x[2], 2)
                wait(pe, "q_taken", 2 * (g + 1))
                project(g, 1, "k_done")
                experts(x[2], 2, 0)
                values(s, 1)
                wait(pe, "x2_lo_done", nx)
                transpose_norm2(nx, 0)
                wait(pe, "k_taken", 4 * (g + 1))
                project_v(g)
                wait(pe, "logit_taken", nx)
                logits(nx, 0)
                experts(x[2], 2, 1)
                wait(pe, "logit_taken", nx + 1)
                transpose_context(2 * s + 1)
                experts(x[2], 2, 2)
                project_out(2 * s + 1)
                experts(x[2], 2, 3)

            supersteps(pe, superstep)

            scores(S_LAST, 0)
            wait(pe, "x2_lo_done", X[1])
            transpose_norm2(X[1], 1)
            experts(X[0], 0, 0)
            experts(X[0], 0, 1)
            wait(pe, "res_done", T_A)
            logits(X[1], 1)
            experts(X[0], 0, 2)
            experts(X[0], 0, 3)
            transpose_prob(T_A)
            experts(X[1], 1, 0)
            wait(pe, "x2_lo_done", X[2])
            transpose_norm2(X[2], 2)
            experts(X[1], 1, 1)
            wait(pe, "logit_taken", X[2])
            logits(X[2], 2)
            transpose_norm2(Y[0], 0)
            scores(S_LAST, 1)
            values(S_LAST, 0)
            experts(X[1], 1, 2)
            wait(pe, "logit_taken", X[2] + 1)
            transpose_context(T_A)
            experts(X[1], 1, 3)
            project_out(T_A)
            experts(X[2], 2, 0)
            transpose_prob(T_B)
            experts(X[2], 2, 1)
            wait(pe, "res_done", T_B)
            logits(Y[0], 0)
            transpose_norm2(Y[1], 1)
            values(S_LAST, 1)
            experts(X[2], 2, 2)
            wait(pe, "logit_taken", Y[1])
            logits(Y[1], 1)
            experts(X[2], 2, 3)
            wait(pe, "logit_taken", Y[2])
            transpose_context(T_B)
            experts(Y[0], 0, 0)
            project_out(T_B)
            for c in (1, 2, 3):
                experts(Y[0], 0, c)
            wait(pe, "x2_lo_done", Y[2])
            transpose_norm2(Y[2], 2)
            experts(Y[1], 1, 0)
            experts(Y[1], 1, 1)
            wait(pe, "res_done", T_B + 1)
            logits(Y[2], 2)
            transpose_norm2(Z, 0)
            experts(Y[1], 1, 2)
            experts(Y[1], 1, 3)
            wait(pe, "logit_taken", Z)
            logits(Z, 0)
            for c in range(CH):
                experts(Y[2], 2, c)
            for c in range(CH):
                experts(Z, 0, c)


def kernel(x, txt, L0_tok_W_lin, L0_tok_b_lin, L0_tok_class_token, L0_tok_position_embeddings,
           L0_attn_Wq, L0_attn_Wk, L0_attn_Wv, L0_attn_Wo, L0_ffn_gate_w, L0_ffn_expert_w):
    import numpy as np
    import concourse.bacc as bacc
    from concourse.bass_utils import run_bass_kernel_spmd

    def chunks(a):
        a = np.asarray(a)
        return np.ascontiguousarray(a.reshape(-1, P, a.shape[-1]).transpose(1, 0, 2))

    x, txt = np.asarray(x), np.asarray(txt)
    xT = x.reshape(NG, GB, 3, 6, 16, 6, 16).transpose(0, 2, 4, 6, 1, 3, 5).reshape(NG, KF, P, GB * NPATCH)
    pos = np.asarray(L0_tok_position_embeddings)[0]
    text_in = txt[:, :TXT_WIN].reshape(PAIRS, 2, TXT_WIN, D).transpose(1, 2, 0, 3).reshape(2, TXT_WIN, PAIRS * D)
    rest = txt[:, TXT_WIN:].reshape(NREST, D)
    wv = np.asarray(L0_attn_Wv).reshape(D, 2, 2, 4, DH).transpose(0, 1, 3, 2, 4).reshape(D, D)
    wo = np.asarray(L0_attn_Wo).reshape(2, 2, 4, DH, D).transpose(1, 0, 2, 3, 4).reshape(D, D)
    heads = (np.arange(P)[:, None] % WIN // DH == np.arange(4)[None]).astype(np.float32)
    consts = np.concatenate([np.eye(P, dtype=np.float32), heads,
                             np.tile(np.arange(NE, dtype=np.float32), (P, 1))], axis=1)
    ins = {
        "xT": np.ascontiguousarray(xT.transpose(0, 2, 1, 3)),
        "wlinT": chunks(np.asarray(L0_tok_W_lin).T),
        "embT": chunks(np.concatenate([pos, np.asarray(L0_tok_b_lin)[None],
                                       np.asarray(L0_tok_class_token)[0]]).T),
        "txt_win": np.ascontiguousarray(text_in),
        "rest": np.ascontiguousarray(rest[:RT * P].reshape(RT, P, D).transpose(1, 0, 2).reshape(P, RT * D)),
        "rest_last": np.ascontiguousarray(rest[RT * P:]),
        "wqkvo": np.ascontiguousarray(np.stack([chunks(w) for w in (L0_attn_Wq, L0_attn_Wk, wv, wo)], axis=1)),
        "gateT": chunks(np.asarray(L0_ffn_gate_w).T),
        "expT": chunks(np.asarray(L0_ffn_expert_w).transpose(2, 0, 1).reshape(D, NE * D)),
        "consts": consts,
    }
    outs = {"out_win": (P, PAIRS * D), "out_rest": (P, RT * D), "out_rest_last": (RLAST, D)}
    nc = bacc.Bacc("TRN2", target_bir_lowering=False, num_devices=1)
    args = [nc.dram_tensor(n, a.shape, F32, kind="ExternalInput").ap() for n, a in ins.items()]
    args += [nc.dram_tensor(n, s, F32, kind="ExternalOutput").ap() for n, s in outs.items()]
    fusion_kernel(nc, *args)
    got = run_bass_kernel_spmd(nc, [ins], core_ids=[0]).results[0]

    w = got["out_win"].reshape(2, WIN, PAIRS, D).transpose(2, 0, 1, 3).reshape(B, WIN, D)
    r = np.concatenate([got["out_rest"].reshape(P, RT, D).transpose(1, 0, 2).reshape(RT * P, D),
                        got["out_rest_last"]]).reshape(B, S - WIN, D)
    return np.concatenate([w[:, NPATCH:NPATCH + 1], w[:, :NPATCH], w[:, NPATCH + 1:], r], axis=1)
```
